# Optimizing a Trainium2 kernel written in Bass

```python
import numpy as np
import jax
import jax.numpy as jnp

def _softmax(x, axis=-1):
    return jax.nn.softmax(x, axis=axis)

def _gelu(x):
    return jax.nn.gelu(x, approximate=True)

def _silu(x):
    return jax.nn.silu(x)

def _sigmoid(x):
    return jax.nn.sigmoid(x)

def _layernorm(x, axis=-1, eps=1e-05):
    m = jnp.mean(x, axis=axis, keepdims=True)
    v = jnp.var(x, axis=axis, keepdims=True)
    return (x - m) / jnp.sqrt(v + eps)

def _scatter_add(tgt, idx, src, axis=0):
    return tgt.at[idx].add(src)

def _segment_sum(src, seg, n):
    return jax.ops.segment_sum(src, seg, n)
kernel_name = 'mk_macaron_d1_jaxref_r4_1c4d3f'

def setup_inputs(seed: int=0):
    np.random.seed(seed)
    _w = jnp.asarray

    def _L0_attn_setup():
        import jax, jax.numpy as jnp
        import numpy as np
        N_HEAD = 16
        WINDOW = 128
        CAUSAL = False

        def _window_attention(x, w_in, b_in, w_out, b_out):
            B, T, D = x.shape
            H = N_HEAD
            hd = D // H
            scale = 1.0 / jnp.sqrt(jnp.float32(hd))
            qkv = jnp.einsum('btd,ed->bte', x, w_in) + b_in
            q, k, v = jnp.split(qkv, 3, axis=-1)
            q = q.reshape(B, T, H, hd).transpose(0, 2, 1, 3)
            k = k.reshape(B, T, H, hd).transpose(0, 2, 1, 3)
            v = v.reshape(B, T, H, hd).transpose(0, 2, 1, 3)
            scores = jnp.einsum('bhqd,bhkd->bhqk', q, k) * scale
            idx = jnp.arange(T)
            diff = idx[:, None] - idx[None, :]
            if CAUSAL:
                allowed = (diff >= 0) & (diff <= WINDOW)
            else:
                allowed = jnp.abs(diff) <= WINDOW
            NEG = jnp.float32(-1e+30)
            scores = jnp.where(allowed[None, None, :, :], scores, NEG)
            attn = jax.nn.softmax(scores, axis=-1)
            ctx = jnp.einsum('bhqk,bhkd->bhqd', attn, v)
            ctx = ctx.transpose(0, 2, 1, 3).reshape(B, T, D)
            out = jnp.einsum('btd,ed->bte', ctx, w_out) + b_out
            return x + out
        key = jax.random.key(seed)
        ks = jax.random.split(key, 5)
        B, T, D = (1, 1024, 256)
        x = jax.random.normal(ks[0], (B, T, D), dtype=jnp.float32)
        w_in = jax.random.normal(ks[1], (3 * D, D), dtype=jnp.float32) * 0.02
        b_in = jax.random.normal(ks[2], (3 * D,), dtype=jnp.float32) * 0.02
        w_out = jax.random.normal(ks[3], (D, D), dtype=jnp.float32) * 0.02
        b_out = jax.random.normal(ks[4], (D,), dtype=jnp.float32) * 0.02
        return {'x': x, 'w_in': w_in, 'b_in': b_in, 'w_out': w_out, 'b_out': b_out}
    _L0_attn_in = _L0_attn_setup()

    def _L0_ffn_setup():
        import jax, jax.numpy as jnp
        import numpy as np
        H = 256
        I = 512
        E = 32
        B, S = (4, 512)

        def _grouped_mm(a, w, group_sizes):
            return jax.lax.ragged_dot(a, w, group_sizes)

        def _swiglu(x, gw, uw, dw):
            return jax.nn.silu(x @ gw) * (x @ uw) @ dw
        key = jax.random.key(seed)
        ks = jax.random.split(key, 8)
        scale = 0.02
        inp = {'hidden_states': jax.random.normal(ks[0], (B, S, H), dtype=jnp.float32), 'gate_w': jax.random.normal(ks[1], (H, E), dtype=jnp.float32) * scale, 'shared_gate_w': jax.random.normal(ks[2], (H, I), dtype=jnp.float32) * scale, 'shared_up_w': jax.random.normal(ks[3], (H, I), dtype=jnp.float32) * scale, 'shared_down_w': jax.random.normal(ks[4], (I, H), dtype=jnp.float32) * scale, 'routed_gate_w': jax.random.normal(ks[5], (E, H, I), dtype=jnp.float32) * scale, 'routed_up_w': jax.random.normal(ks[6], (E, H, I), dtype=jnp.float32) * scale, 'routed_down_w': jax.random.normal(ks[7], (E, I, H), dtype=jnp.float32) * scale}
        return inp
    _L0_ffn_in = _L0_ffn_setup()
    _d = {'L0_attn_x': _L0_attn_in['x'], 'L0_attn_w_in': _L0_attn_in['w_in'], 'L0_attn_b_in': _L0_attn_in['b_in'], 'L0_attn_w_out': _L0_attn_in['w_out'], 'L0_attn_b_out': _L0_attn_in['b_out'], 'L0_ffn_gate_w': _L0_ffn_in['gate_w'], 'L0_ffn_shared_gate_w': _L0_ffn_in['shared_gate_w'], 'L0_ffn_shared_up_w': _L0_ffn_in['shared_up_w'], 'L0_ffn_shared_down_w': _L0_ffn_in['shared_down_w'], 'L0_ffn_routed_gate_w': _L0_ffn_in['routed_gate_w'], 'L0_ffn_routed_up_w': _L0_ffn_in['routed_up_w'], 'L0_ffn_routed_down_w': _L0_ffn_in['routed_down_w']}
    _x0 = _d['L0_attn_x']
    _d['L0_attn_x'] = jax.random.normal(jax.random.fold_in(jax.random.key(seed), 1), (32, 512, 256), dtype=_x0.dtype)
    del _x0
    return _d

def reference(L0_attn_x, L0_attn_w_in, L0_attn_b_in, L0_attn_w_out, L0_attn_b_out, L0_ffn_gate_w, L0_ffn_shared_gate_w, L0_ffn_shared_up_w, L0_ffn_shared_down_w, L0_ffn_routed_gate_w, L0_ffn_routed_up_w, L0_ffn_routed_down_w):

    def _L0_attn_ref(x, w_in, b_in, w_out, b_out):
        import jax, jax.numpy as jnp
        import numpy as np
        N_HEAD = 16
        WINDOW = 128
        CAUSAL = False

        def _window_attention(x, w_in, b_in, w_out, b_out):
            B, T, D = x.shape
            H = N_HEAD
            hd = D // H
            scale = 1.0 / jnp.sqrt(jnp.float32(hd))
            qkv = jnp.einsum('btd,ed->bte', x, w_in) + b_in
            q, k, v = jnp.split(qkv, 3, axis=-1)
            q = q.reshape(B, T, H, hd).transpose(0, 2, 1, 3)
            k = k.reshape(B, T, H, hd).transpose(0, 2, 1, 3)
            v = v.reshape(B, T, H, hd).transpose(0, 2, 1, 3)
            scores = jnp.einsum('bhqd,bhkd->bhqk', q, k) * scale
            idx = jnp.arange(T)
            diff = idx[:, None] - idx[None, :]
            if CAUSAL:
                allowed = (diff >= 0) & (diff <= WINDOW)
            else:
                allowed = jnp.abs(diff) <= WINDOW
            NEG = jnp.float32(-1e+30)
            scores = jnp.where(allowed[None, None, :, :], scores, NEG)
            attn = jax.nn.softmax(scores, axis=-1)
            ctx = jnp.einsum('bhqk,bhkd->bhqd', attn, v)
            ctx = ctx.transpose(0, 2, 1, 3).reshape(B, T, D)
            out = jnp.einsum('btd,ed->bte', ctx, w_out) + b_out
            return x + out
        return _window_attention(x, w_in, b_in, w_out, b_out)

    def _L0_ffn_ref(hidden_states, gate_w, shared_gate_w, shared_up_w, shared_down_w, routed_gate_w, routed_up_w, routed_down_w):
        import jax, jax.numpy as jnp
        import numpy as np
        H = 256
        I = 512
        E = 32
        B, S = (4, 512)

        def _grouped_mm(a, w, group_sizes):
            return jax.lax.ragged_dot(a, w, group_sizes)

        def _swiglu(x, gw, uw, dw):
            return jax.nn.silu(x @ gw) * (x @ uw) @ dw
        b, s, h = hidden_states.shape
        x = hidden_states.reshape(-1, h)
        shared_out = _swiglu(x, shared_gate_w, shared_up_w, shared_down_w)
        logits = x @ gate_w
        topk_ids = jnp.argmax(logits, axis=-1)
        topk_val = jnp.max(logits, axis=-1)
        scores = jax.nn.sigmoid(topk_val)[:, None]
        xs = x * scores
        tokens_per_expert = jnp.zeros((E,), jnp.int32).at[topk_ids].add(1)
        order = jnp.argsort(topk_ids)
        sorted_x = xs[order]
        g = _grouped_mm(sorted_x, routed_gate_w, tokens_per_expert)
        u = _grouped_mm(sorted_x, routed_up_w, tokens_per_expert)
        d = _grouped_mm(jax.nn.silu(g) * u, routed_down_w, tokens_per_expert)
        inv = jnp.argsort(order)
        routed_out = d[inv]
        return (shared_out + routed_out).reshape(b, s, h)
    x = L0_attn_x
    x = x + 0.5 * _L0_ffn_ref(_layernorm(x, axis=-1), L0_ffn_gate_w, L0_ffn_shared_gate_w, L0_ffn_shared_up_w, L0_ffn_shared_down_w, L0_ffn_routed_gate_w, L0_ffn_routed_up_w, L0_ffn_routed_down_w)
    x = x + _L0_attn_ref(_layernorm(x, axis=-1), L0_attn_w_in, L0_attn_b_in, L0_attn_w_out, L0_attn_b_out)
    x = x + 0.5 * _L0_ffn_ref(_layernorm(x, axis=-1), L0_ffn_gate_w, L0_ffn_shared_gate_w, L0_ffn_shared_up_w, L0_ffn_shared_down_w, L0_ffn_routed_gate_w, L0_ffn_routed_up_w, L0_ffn_routed_down_w)
    return x

_drawn_inputs = setup_inputs


def setup_inputs(seed=0):
    import zlib

    import numpy as np

    out = dict(_drawn_inputs(seed))
    spreads = {}
    factors = {'L0_attn_w_in': 8.0,
     'L0_attn_b_in': 8.0,
     'L0_attn_w_out': 8.0,
     'L0_attn_b_out': 5.813,
     'L0_ffn_gate_w': 7.45,
     'L0_ffn_shared_gate_w': 3.191,
     'L0_ffn_shared_up_w': 3.156,
     'L0_ffn_shared_down_w': 3.148,
     'L0_ffn_routed_gate_w': 7.368,
     'L0_ffn_routed_up_w': 7.331,
     'L0_ffn_routed_down_w': 7.336}
    for name, (base, spread) in spreads.items():
        noise = np.random.default_rng([zlib.crc32(name.encode()), seed]).standard_normal(out[name].shape)
        drawn = base * np.exp(spread * noise) if base else spread * noise
        out[name] = jnp.asarray(drawn.astype(out[name].dtype))
    for name, factor in factors.items():
        out[name] = (out[name] * factor).astype(out[name].dtype)
    return out
```

```python
from contextlib import ExitStack

import concourse.bass as bass
from concourse import mybir

ALU = mybir.AluOpType
ACT = mybir.ActivationFunctionType
AX = mybir.AxisListType
F32 = mybir.dt.float32
F32R = mybir.dt.float32r
BF16 = mybir.dt.bfloat16
I32 = mybir.dt.int32
U32 = mybir.dt.uint32

P = 128
EPS = 1e-5
WINDOW = 128
NEG = -1e30


class Shapes:

    def __init__(self, x, w_in, gate_w, sg, rg):
        self.B, self.T, self.D = x.shape
        self.N = self.B * self.T
        self.KD = self.D // P
        self.CH = 512
        self.J = self.CH // P
        self.NCH = self.N // self.CH
        self.NTL = self.N // P
        self.E = gate_w.shape[1]
        self.I = sg.shape[1]
        self.KI = self.I // P
        self.NRT = (self.NTL + self.E - 1 + 15) // 16 * 16
        self.H = 16
        self.HD = self.D // self.H


def ds(start, size):
    return bass.ds(start, size)


def positive(value):
    return not isinstance(value, int) or value > 0


def ahead_of_wait(eng, value):
    return value if isinstance(value, int) else eng.to_reg(value)


def hold(eng, passed):
    eng.sem_inc(passed, 1)


def semaphores(nc, ctx):
    held = []

    def taken(name):
        held.append(nc.alloc_semaphore(name))
        return held[-1]

    def give_back():
        nc.clear_and_free_semaphores(held)
        nc.all_engine_barrier()

    ctx.callback(give_back)
    return taken


def router(nc, s, tag, x_d, xn_d, gate_w, onehot, top_logit, ident, fill):
    with ExitStack() as ctx:
        taken = semaphores(nc, ctx)

        def sb(name, shape, dt=F32):
            return ctx.enter_context(nc.sbuf_tensor(f"{tag}_{name}", shape, dt))

        def ps(name, shape):
            return ctx.enter_context(nc.psum_tensor(f"{tag}_{name}", shape, F32))

        def sem(name):
            return taken(f"{tag}_{name}")

        J, KD, D, E = s.J, s.KD, s.D, s.E
        gw = sb("gw", [P, KD, E])
        from_e = sb("from_e", [P, E])
        neg_half = sb("neg_half", [P, J])
        x = [sb(f"x{u}", [P, J, D]) for u in range(2)]
        xn = [sb(f"xn{u}", [P, J, D]) for u in range(2)]
        xnT = [sb(f"xnT{u}", [P, KD, s.CH]) for u in range(2)]
        stats = [sb(f"stats{u}", [P, J, 6]) for u in range(2)]
        mv = [sb(f"mv{u}", [P, J, 2]) for u in range(2)]
        vare = [sb(f"vare{u}", [P, J]) for u in range(2)]
        rstd = [sb(f"rstd{u}", [P, J]) for u in range(2)]
        mx = [sb(f"mx{u}", [P, J]) for u in range(2)]
        at_top = [sb(f"at_top{u}", [P, J, E]) for u in range(2)]
        cand = [sb(f"cand{u}", [P, J, E]) for u in range(2)]
        idx = [sb(f"idx{u}", [P, J]) for u in range(2)]
        psT = [ps(f"psT{u}", [P, KD, s.CH]) for u in range(2)]
        psL = [ps(f"psL{u}", [P, 512]) for u in range(2)]

        x_in = [sem(f"x_in{u}") for u in range(2)]
        xn_out = [sem(f"xn_out{u}") for u in range(2)]
        gw_in = sem("gw_in")
        dve_passed = sem("dve_passed")
        consts = sem("consts")
        stat_ok = sem("stat_ok")
        aggr_ok = sem("aggr_ok")
        vare_ok = sem("vare_ok")
        rstd_ok = sem("rstd_ok")
        xn_ok = sem("xn_ok")
        t_ok = sem("t_ok")
        xnT_ok = sem("xnT_ok")
        lg_ps = sem("lg_ps")
        lg_ok = sem("lg_ok")
        mx_ok = sem("mx_ok")
        ix_ok = sem("ix_ok")
        idx_ok = sem("idx_ok")
        oh_ok = sem("oh_ok")

        x_v = x_d.rearrange("(c j p) d -> c p j d", j=J, p=P)
        xn_v = xn_d.rearrange("(c j p) d -> c p j d", j=J, p=P)

        with nc.Block() as block:
            @block.sync
            def _(sp):
                sp.dma_start(gw[:], gate_w.rearrange("(k p) e -> p k e", p=P)).then_inc(gw_in, 16)

                def load(c, u):
                    sp.dma_start(x[u][:], x_v[ds(c, 1)].rearrange("o p j d -> (o p) j d")).then_inc(x_in[u], 16)

                def store(c, u):
                    sp.wait_ge(xn_ok, c + 1)
                    sp.dma_start(xn_v[ds(c, 1)].rearrange("o p j d -> (o p) j d"), xn[u][:]).then_inc(xn_out[u], 16)

                def clear(i):
                    if fill:
                        rows, zeros, filled = fill
                        part = rows.rearrange("(g p r) d -> g p r d", g=s.NCH // 2, p=P)
                        sp.dma_start(part[ds(i, 1)].rearrange("o p r d -> (o p) r d"),
                                     zeros[:].unsqueeze(1).broadcast_to([P, part.shape[2], D])).then_inc(filled, 16)

                load(0, 0)
                load(1, 1)
                with sp.Fori(0, s.NCH // 2 - 1) as i:
                    for u in range(2):
                        store(2 * i + u, u)
                        load(2 * i + 2 + u, u)
                    clear(i)
                for u in range(2):
                    store(s.NCH - 2 + u, u)
                clear(s.NCH // 2 - 1)
                for u in range(2):
                    sp.wait_ge(xn_out[u], 16 * (s.NCH // 2))

            @block.gpsimd
            def _(pool):
                pool.memset(neg_half[:], -0.5).then_inc(consts, 1)
                pool.iota(from_e[:], [[1, E]], base=-E, channel_multiplier=0,
                          allow_small_or_imprecise_dtypes=True).then_inc(consts, 1)
                pool.wait_ge(consts, 2)
                with pool.Fori(0, s.NCH // 2) as i:
                    for u in range(2):
                        pool.wait_ge(vare_ok, 2 * i + u + 1)
                        pool.tensor_tensor(rstd[u][:], vare[u][:], neg_half[:], ALU.pow).then_inc(rstd_ok, 1)

            @block.vector
            def _(dve):
                def norm(c, u, i):
                    dve.wait_ge(x_in[u], 16 * i + 16)
                    for j in range(J):
                        last = dve.bn_stats(stats[u][:, j, :], x[u][:, j, :])
                    last.then_inc(stat_ok, 1)
                    dve.wait_ge(stat_ok, c + 1)
                    hold(dve, dve_passed)
                    for j in range(J):
                        last = dve.bn_aggr(mv[u][:, j, :], stats[u][:, j, :])
                    last.then_inc(aggr_ok, 1)
                    dve.wait_ge(aggr_ok, c + 1)
                    dve.tensor_scalar(vare[u][:], mv[u][:, :, 1], EPS, None, ALU.add).then_inc(vare_ok, 1)

                def scale(c, u, i):
                    dve.wait_ge(rstd_ok, c + 1)
                    if positive(i):
                        dve.wait_ge(xn_out[u], 16 * i)
                        dve.wait_ge(t_ok, c - 1)
                    for j in range(J):
                        last = dve.tensor_scalar(xn[u][:, j, :], x[u][:, j, :], mv[u][:, j, 0:1], rstd[u][:, j:j + 1],
                                                 ALU.subtract, ALU.mult)
                    last.then_inc(xn_ok, 1)

                def route(c, u):
                    dve.wait_ge(lg_ps, c + 1)
                    lg = psL[u][:, 0:J * E].rearrange("p (j e) -> p j e", j=J)
                    dve.tensor_reduce(mx[u][:], lg, AX.X, ALU.max).then_inc(mx_ok, 1)
                    dve.wait_ge(mx_ok, c + 1)
                    dve.tensor_tensor(at_top[u][:], lg, mx[u][:].unsqueeze(2).broadcast_to([P, J, E]),
                                      ALU.is_equal).then_inc(lg_ok, 1)
                    dve.wait_ge(lg_ok, c + 1)
                    dve.tensor_tensor(cand[u][:], at_top[u][:], from_e[:].unsqueeze(1).broadcast_to([P, J, E]),
                                      ALU.mult).then_inc(ix_ok, 1)
                    dve.wait_ge(ix_ok, c + 1)
                    dve.tensor_reduce(idx[u][:], cand[u][:], AX.X, ALU.min).then_inc(idx_ok, 1)
                    dve.tensor_copy(top_logit[:, ds(c * J, J)], mx[u][:])
                    dve.wait_ge(idx_ok, c + 1)
                    dve.tensor_tensor(onehot[:, ds(c * J, J), :], from_e[:].unsqueeze(1).broadcast_to([P, J, E]),
                                      idx[u][:].unsqueeze(2).broadcast_to([P, J, E]), ALU.is_equal).then_inc(oh_ok, 1)

                dve.wait_ge(consts, 2)
                for c in range(4):
                    norm(c, c % 2, c // 2)
                    if c == 3:
                        route(0, 0)
                    scale(c, c % 2, c // 2)
                with dve.Fori(2, s.NCH // 2) as i:
                    for u in range(2):
                        norm(2 * i + u, u, i)
                        route(2 * i + u - 3, 1 - u)
                        scale(2 * i + u, u, i)
                for c in range(s.NCH - 3, s.NCH):
                    route(c, c % 2)
                dve.wait_ge(oh_ok, s.NCH)

            @block.scalar
            def _(act):
                def evac(c, u):
                    act.wait_ge(t_ok, c + 1)
                    if positive(c - 1):
                        act.wait_ge(lg_ps, c - 1)
                    for k in range(KD):
                        last = act.copy(xnT[u][:, k, :], psT[u][:, k, :])
                    last.then_inc(xnT_ok, 1)

                for u in range(2):
                    evac(u, u)
                with act.Fori(1, s.NCH // 2) as i:
                    for u in range(2):
                        evac(2 * i + u, u)

            @block.tensor
            def _(pe):
                def turn(c, u):
                    pe.wait_ge(xn_ok, c + 1)
                    if positive(c - 1):
                        pe.wait_ge(xnT_ok, c - 1)
                    for k in range(KD):
                        for j in range(J):
                            last = pe.transpose(psT[u][:, k, j * P:(j + 1) * P], xn[u][:, j, k * P:(k + 1) * P], ident[:])
                    last.then_inc(t_ok, 1)

                def logits(c, u):
                    pe.wait_ge(xnT_ok, c + 1)
                    if positive(c - 1):
                        pe.wait_ge(lg_ok, c - 1)
                    for j in range(J):
                        for k in range(KD):
                            last = pe.matmul(psL[u][:, j * E:(j + 1) * E], xnT[u][:, k, j * P:(j + 1) * P], gw[:, k, :],
                                             start=(k == 0), stop=(k == KD - 1))
                    last.then_inc(lg_ps, 1)

                pe.wait_ge(gw_in, 16)
                turn(0, 0)
                turn(1, 1)
                logits(0, 0)
                with pe.Fori(1, s.NCH // 2) as i:
                    turn(2 * i, 0)
                    logits(2 * i - 1, 1)
                    turn(2 * i + 1, 1)
                    logits(2 * i, 0)
                logits(s.NCH - 1, 1)


def places(nc, s, tag, onehot, top_logit, score, place, tile_expert, expert_end, ones_bf, upper_bf):
    with ExitStack() as ctx:
        taken = semaphores(nc, ctx)

        def sb(name, shape, dt=F32):
            return ctx.enter_context(nc.sbuf_tensor(f"{tag}_{name}", shape, dt))

        def sem(name):
            return taken(f"{tag}_{name}")

        E, NTL = s.E, s.NTL
        G = 512 // E
        NG = NTL // G
        count = sb("count", [P, E, NTL])
        incl = sb("incl", [P, E, NTL])
        zero = sb("zero", [P, 1])
        n_e = sb("n_e", [P, E])
        n_i = sb("n_i", [P, E], I32)
        t_i = sb("t_i", [P, E], I32)
        t_e = sb("t_e", [P, E])
        cum = sb("cum", [P, E])
        shift = sb("shift", [P, E])
        tmp = sb("tmp", [P, E])
        row = [sb(f"row{u}", [P, G, E]) for u in range(2)]
        hit = [sb(f"hit{u}", [P, G, E]) for u in range(2)]
        place_f = sb("place_f", [P, NTL])
        tio = sb("tio", [1, s.NRT])
        cmp = sb("cmp", [1, s.NRT, E])
        te = sb("te", [1, s.NRT])
        te2 = sb("te2", [1, s.NRT])
        banks = [ctx.enter_context(nc.psum_tensor(f"{tag}_bank{g}", [P, G, E], F32)) for g in range(NG)]

        cnt_ps = sem("cnt_ps")
        cnt_ok = sem("cnt_ok")
        rank_ps = sem("rank_ps")
        chain = sem("chain")
        tio_ok = sem("tio_ok")
        score_ok = sem("score_ok")

        with nc.Block() as block:
            @block.tensor
            def _(pe):
                for g in range(NG):
                    pe.matmul(banks[g][:], ones_bf[:], onehot[:, g * G:(g + 1) * G, :], start=True,
                              stop=True).then_inc(cnt_ps, 1)
                for g in range(NG):
                    pe.wait_ge(cnt_ok, g + 1)
                    pe.matmul(banks[g][:], upper_bf[:], onehot[:, g * G:(g + 1) * G, :], start=True,
                              stop=True).then_inc(rank_ps, 1)

            @block.gpsimd
            def _(pool):
                pool.iota(tio[:], [[1, s.NRT]], base=0, channel_multiplier=0,
                          allow_small_or_imprecise_dtypes=True).then_inc(tio_ok, 1)

            @block.scalar
            def _(act):
                act.activation(score[:], top_logit[:], ACT.Sigmoid).then_inc(score_ok, 1)
                act.wait_ge(score_ok, 1)

            @block.vector
            def _(dve):
                done = [0]

                def step(ins):
                    done[0] += 1
                    ins.then_inc(chain, 1)
                    dve.wait_ge(chain, done[0])

                step(dve.memset(zero[:], 0.0))
                for g in range(NG):
                    dve.wait_ge(cnt_ps, g + 1)
                    dve.tensor_copy(count[:, :, g * G:(g + 1) * G], banks[g][:].rearrange("p t e -> p e t")).then_inc(cnt_ok, 1)
                dve.wait_ge(cnt_ok, NG)
                flat = "p e t -> p (e t)"
                step(dve.tensor_tensor_scan(incl[:].rearrange(flat), count[:].rearrange(flat),
                                            zero[:].broadcast_to([P, E * NTL]), 0.0, ALU.add, ALU.add))
                step(dve.tensor_copy(n_e[:, 0:1], incl[:, 0:1, NTL - 1]))
                step(dve.tensor_tensor(n_e[:, 1:E], incl[:, 1:E, NTL - 1], incl[:, 0:E - 1, NTL - 1], ALU.subtract))
                step(dve.tensor_scalar(n_i[:], n_e[:], float(P - 1), None, ALU.add))
                step(dve.tensor_scalar(t_i[:], n_i[:], 7, None, ALU.arith_shift_right))
                step(dve.tensor_copy(t_e[:], t_i[:]))
                step(dve.tensor_tensor_scan(cum[:], t_e[:], zero[:].broadcast_to([P, E]), 0.0, ALU.add, ALU.add))
                step(dve.tensor_tensor(tmp[:], cum[:], t_e[:], ALU.subtract))
                step(dve.scalar_tensor_tensor(tmp[:], tmp[:], float(P), n_e[:], ALU.mult, ALU.add))
                step(dve.tensor_tensor(shift[:], tmp[:], incl[:, :, NTL - 1], ALU.subtract))
                step(dve.tensor_tensor(incl[:], incl[:], count[:], ALU.subtract))
                step(dve.tensor_tensor(incl[:], incl[:], shift[:].unsqueeze(2).broadcast_to([P, E, NTL]), ALU.add))
                for g in range(NG):
                    dve.wait_ge(rank_ps, g + 1)
                    step(dve.tensor_tensor(row[g % 2][:], banks[g][:], incl[:, :, g * G:(g + 1) * G].rearrange("p e t -> p t e"), ALU.add))
                    step(dve.tensor_tensor(hit[g % 2][:], row[g % 2][:], onehot[:, g * G:(g + 1) * G, :], ALU.mult))
                    step(dve.tensor_reduce(place_f[:, g * G:(g + 1) * G], hit[g % 2][:], AX.X, ALU.add))
                step(dve.tensor_copy(place[:], place_f[:]))
                dve.wait_ge(tio_ok, 1)
                step(dve.tensor_tensor(cmp[:], cum[0:1, :].unsqueeze(1).broadcast_to([1, s.NRT, E]),
                                       tio[:].unsqueeze(2).broadcast_to([1, s.NRT, E]), ALU.is_le))
                step(dve.tensor_reduce(te[:], cmp[:], AX.X, ALU.add))
                step(dve.tensor_scalar(te2[:], te[:], float(E - 1), None, ALU.min))
                step(dve.tensor_copy(tile_expert[:], te2[:]))
                step(dve.tensor_scalar(expert_end[:], cum[0:1, :], 1.0, None, ALU.add))


def shared_ffn(nc, s, tag, x_d, xn_d, y_d, grouped_d, gate_w, up_w, down_w, score, place, ident, filled):
    with ExitStack() as ctx:
        taken = semaphores(nc, ctx)

        def sb(name, shape, dt=F32):
            return ctx.enter_context(nc.sbuf_tensor(f"{tag}_{name}", shape, dt))

        def ps(name, shape):
            return ctx.enter_context(nc.psum_tensor(f"{tag}_{name}", shape, F32))

        def sem(name):
            return taken(f"{tag}_{name}")

        J, KD, D, KI, I, CH = s.J, s.KD, s.D, s.KI, s.I, s.CH
        wg_raw = sb("wg_raw", [P, KD, I])
        wu_raw = sb("wu_raw", [P, KD, I])
        wd_raw = sb("wd_raw", [P, KI, D])
        raws = [wg_raw, wu_raw, wd_raw]
        w_hi = [sb(f"w_hi{n}", list(r.shape), F32R) for n, r in enumerate(raws)]
        w_lo = [sb(f"w_lo{n}", list(r.shape), F32R) for n, r in enumerate(raws)]
        x = [sb(f"x{u}", [P, J, D]) for u in range(2)]
        xn = [sb(f"xn{u}", [P, J, D]) for u in range(2)]
        xs = [sb(f"xs{u}", [P, J, D]) for u in range(2)]
        place_c = [sb(f"place_c{u}", [P, J], I32) for u in range(2)]
        y = [sb(f"y{u}", [P, J, D]) for u in range(2)]
        xT_hi = [sb(f"xT_hi{u}", [P, KD, CH], F32R) for u in range(2)]
        xT_lo = [sb(f"xT_lo{u}", [P, KD, CH], F32R) for u in range(2)]
        act_g = [sb(f"act_g{m}", [P, CH]) for m in range(2)]
        h = [sb(f"h{m}", [P, CH]) for m in range(2)]
        h_hi = [sb(f"h_hi{u}", [P, KI, CH], F32R) for u in range(2)]
        h_lo = [sb(f"h_lo{u}", [P, KI, CH], F32R) for u in range(2)]
        psT = [ps(f"psT{k}", [P, CH]) for k in range(KD)]
        psG = [ps(f"psG{m}", [P, CH]) for m in range(2)]
        psU = [ps(f"psU{m}", [P, CH]) for m in range(2)]
        psO = [ps(f"psO{m}", [P, 512]) for m in range(2)]

        w_in = sem("w_in")
        w_ok = sem("w_ok")
        x_in = [sem(f"x_in{u}") for u in range(2)]
        xn_in = [sem(f"xn_in{u}") for u in range(2)]
        y_out = [sem(f"y_out{u}") for u in range(2)]
        place_ok = sem("place_ok")
        pool_passed = sem("pool_passed")
        xs_ok = sem("xs_ok")
        xs_out = [sem(f"xs_out{u}") for u in range(2)]
        t_ok = sem("t_ok")
        hi_ok = sem("hi_ok")
        lo_ok = sem("lo_ok")
        g_ps = sem("g_ps")
        gu_ps = sem("gu_ps")
        act_ok = sem("act_ok")
        h_ok = sem("h_ok")
        hhi_ok = sem("hhi_ok")
        hlo_ok = sem("hlo_ok")
        o_ps = sem("o_ps")
        y_ok = sem("y_ok")

        def view(d):
            return d.rearrange("(c j p) d -> c p j d", j=J, p=P)

        def chunk(v, c):
            return v[ds(c, 1)].rearrange("o p j d -> (o p) j d")

        x_v, xn_v, y_v = view(x_d), view(xn_d), view(y_d)
        NIT = s.NCH // 2

        with nc.Block() as block:
            @block.sync
            def _(sp):
                for raw, w in ((wg_raw, gate_w), (wu_raw, up_w), (wd_raw, down_w)):
                    sp.dma_start(raw[:], w.rearrange("(k p) n -> p k n", p=P)).then_inc(w_in, 16)

                def load(c, u):
                    sp.dma_start(xn[u][:], chunk(xn_v, c)).then_inc(xn_in[u], 16)
                    sp.dma_start(x[u][:], chunk(x_v, c)).then_inc(x_in[u], 16)

                def store(c, u):
                    sp.wait_ge(y_ok, J * c + J)
                    sp.dma_start(chunk(y_v, c), y[u][:]).then_inc(y_out[u], 16)

                load(0, 0)
                load(1, 1)
                with sp.Fori(1, NIT) as i:
                    for u in range(2):
                        store(2 * i - 2 + u, u)
                        sp.wait_ge(t_ok, 2 * i - 1 + u)
                        sp.wait_ge(xs_ok, 2 * i - 1 + u)
                        load(2 * i + u, u)
                for u in range(2):
                    store(s.NCH - 2 + u, u)
                for u in range(2):
                    sp.wait_ge(y_out[u], 16 * NIT)

            @block.gpsimd
            def _(pool):
                def scatter(c, u, i):
                    pool.wait_ge(xs_ok, c + 1)
                    pool.wait_ge(place_ok, c + 1)
                    hold(pool, pool_passed)
                    for j in range(J):
                        pool.indirect_dma_start(
                            out=grouped_d, out_offset=bass.IndirectOffsetOnAxis(ap=place_c[u][:, j:j + 1], axis=0),
                            in_=xs[u][:, j, :], in_offset=None).then_inc(xs_out[u], 16)

                def scale_tokens(c, u, i):
                    pool.wait_ge(xn_in[u], 16 * i + 16)
                    if positive(i):
                        pool.wait_ge(xs_out[u], 16 * J * i)
                    pool.tensor_copy(place_c[u][:], place[:, ds(c * J, J)]).then_inc(place_ok, 1)
                    pool.tensor_tensor(xs[u][:], xn[u][:], score[:, ds(c * J, J)].unsqueeze(2).broadcast_to([P, J, D]),
                                       ALU.mult).then_inc(xs_ok, 1)

                for u in range(2):
                    scale_tokens(u, u, 0)
                    if u == 0:
                        pool.wait_ge(filled, 16 * (s.NCH // 2))
                    scatter(u, u, 0)
                with pool.Fori(1, NIT) as i:
                    for u in range(2):
                        scale_tokens(2 * i + u, u, i)
                        scatter(2 * i + u, u, i)
                for u in range(2):
                    pool.wait_ge(xs_out[u], 16 * J * NIT)

            @block.scalar
            def _(act):
                def hi_of(c, u):
                    act.wait_ge(t_ok, c + 1)
                    if positive(KI * c - KI):
                        act.wait_ge(gu_ps, KI * c - KI)
                    for k in range(KD):
                        last = act.copy(xT_hi[u][:, k, :], psT[k][:])
                    last.then_inc(hi_ok, 1)

                def slices(c, u, last):
                    for m in range(KI):
                        act.wait_ge(g_ps, KI * c + m + 1)
                        if positive(KI * c + m - 1):
                            act.wait_ge(h_ok, KI * c + m - 1)
                        act.activation(act_g[m % 2][:], psG[m % 2][:], ACT.Silu).then_inc(act_ok, 1)
                        act.wait_ge(h_ok, KI * c + m + 1)
                        if m == 0 and positive(J * c - J):
                            act.wait_ge(o_ps, J * c - J)
                        act.copy(h_hi[u][:, m, :], h[m % 2][:]).then_inc(hhi_ok, 1)
                        if m == KI - 2 and not last:
                            hi_of(c + 1, 1 - u)

                hi_of(0, 0)
                slices(0, 0, False)
                slices(1, 1, False)
                with act.Fori(1, NIT - 1) as i:
                    for u in range(2):
                        slices(2 * i + u, u, False)
                slices(s.NCH - 2, 0, False)
                slices(s.NCH - 1, 1, True)

            @block.vector
            def _(dve):
                dve.wait_ge(w_in, 16 * 3)
                for n in range(3):
                    dve.tensor_copy(w_hi[n][:], raws[n][:]).then_inc(w_ok, 1)
                dve.wait_ge(w_ok, 3)
                for n in range(3):
                    dve.tensor_tensor(w_lo[n][:], raws[n][:], w_hi[n][:].bitcast(F32), ALU.subtract).then_inc(w_ok, 1)

                def lo_of(c, u):
                    dve.wait_ge(hi_ok, c + 1)
                    for k in range(KD):
                        last = dve.tensor_tensor(xT_lo[u][:, k, :], psT[k][:], xT_hi[u][:, k, :].bitcast(F32), ALU.subtract)
                    last.then_inc(lo_ok, 1)

                def add(c, j, u, i):
                    dve.wait_ge(o_ps, J * c + j + 1)
                    if j == 0:
                        dve.wait_ge(x_in[u], 16 * i + 16)
                        if positive(i):
                            dve.wait_ge(y_out[u], 16 * i)
                    dve.scalar_tensor_tensor(y[u][:, j, :], psO[j % 2][:, 0:D], 0.5, x[u][:, j, :], ALU.mult,
                                             ALU.add).then_inc(y_ok, 1)

                def slices(c, u, i, last):
                    for m in range(KI):
                        dve.wait_ge(act_ok, KI * c + m + 1)
                        dve.wait_ge(gu_ps, KI * c + m + 1)
                        if positive(KI * c + m - 1):
                            dve.wait_ge(hlo_ok, KI * c + m - 1)
                        dve.tensor_tensor(h[m % 2][:], act_g[m % 2][:], psU[m % 2][:], ALU.mult).then_inc(h_ok, 1)
                        dve.wait_ge(hhi_ok, KI * c + m + 1)
                        dve.tensor_tensor(h_lo[u][:, m, :], h[m % 2][:], h_hi[u][:, m, :].bitcast(F32),
                                          ALU.subtract).then_inc(hlo_ok, 1)
                        if m == 0 and positive(c):
                            for j in range(J):
                                add(c - 1, j, 1 - u, i - 1 + u)
                        if m == KI - 2 and not last:
                            lo_of(c + 1, 1 - u)

                lo_of(0, 0)
                slices(0, 0, 0, False)
                slices(1, 1, 0, False)
                with dve.Fori(1, NIT - 1) as i:
                    for u in range(2):
                        slices(2 * i + u, u, i, False)
                slices(s.NCH - 2, 0, NIT - 1, False)
                slices(s.NCH - 1, 1, NIT - 1, True)
                for j in range(J):
                    add(s.NCH - 1, j, 1, NIT - 1)

            @block.tensor
            def _(pe):
                def turn(c, u, i):
                    pe.wait_ge(xn_in[u], 16 * i + 16)
                    if positive(c):
                        pe.wait_ge(lo_ok, c)
                    for k in range(KD):
                        for j in range(J):
                            last = pe.transpose(psT[k][:, j * P:(j + 1) * P], xn[u][:, j, k * P:(k + 1) * P], ident[:])
                    last.then_inc(t_ok, 1)

                def down(c, u):
                    pe.wait_ge(hlo_ok, KI * c + KI)
                    for j in range(J):
                        if positive(J * c + j - 1):
                            pe.wait_ge(y_ok, J * c + j - 1)
                        js = slice(j * P, (j + 1) * P)
                        g = 0
                        for k in range(KI):
                            for t, w in ((h_hi, w_hi), (h_hi, w_lo), (h_lo, w_hi)):
                                last = pe.matmul(psO[j % 2][:, 0:D], t[u][:, k, js], w[2][:, k, :], start=(g == 0),
                                                 stop=(g == 3 * KI - 1))
                                g += 1
                        last.then_inc(o_ps, 1)

                def slices(c, u, i, last_chunk):
                    pe.wait_ge(lo_ok, c + 1)
                    for m in range(KI):
                        if positive(KI * c + m - 1):
                            pe.wait_ge(h_ok, KI * c + m - 1)
                        ms = slice(m * P, (m + 1) * P)
                        for n, dst, done in ((0, psG[m % 2], g_ps), (1, psU[m % 2], gu_ps)):
                            g = 0
                            for k in range(KD):
                                for w, t in ((w_hi, xT_hi), (w_hi, xT_lo), (w_lo, xT_hi)):
                                    last = pe.matmul(dst[:], w[n][:, k, ms], t[u][:, k, :], start=(g == 0),
                                                     stop=(g == 3 * KD - 1))
                                    g += 1
                            last.then_inc(done, 1)
                        if m == 0 and positive(c):
                            down(c - 1, 1 - u)
                        if m == KI - 2 and not last_chunk:
                            turn(c + 1, 1 - u, i + u)

                turn(0, 0, 0)
                pe.wait_ge(w_ok, 6)
                slices(0, 0, 0, False)
                slices(1, 1, 0, False)
                with pe.Fori(1, NIT - 1) as i:
                    for u in range(2):
                        slices(2 * i + u, u, i, False)
                slices(s.NCH - 2, 0, NIT - 1, False)
                slices(s.NCH - 1, 1, NIT - 1, True)
                down(s.NCH - 1, 1)


def routed_ffn(nc, s, tag, grouped_d, routed_d, gate_w, up_w, down_w, tile_expert, expert_end, ident):
    with ExitStack() as ctx:
        taken = semaphores(nc, ctx)

        def sb(name, shape, dt=F32):
            return ctx.enter_context(nc.sbuf_tensor(f"{tag}_{name}", shape, dt))

        def ps(name, shape):
            return ctx.enter_context(nc.psum_tensor(f"{tag}_{name}", shape, F32))

        def sem(name):
            return taken(f"{tag}_{name}")

        KD, D, KI, I, E, NRT = s.KD, s.D, s.KI, s.I, s.E, s.NRT
        WG, WU, WD, WN = 0, KD * I, 2 * KD * I, 2 * KD * I + KI * D
        HALF = WN // 2
        raw = [sb(f"raw{v}", [P, WN]) for v in range(2)]
        w_hi = sb("w_hi", [P, 2 * WN], F32R)
        w_lo = sb("w_lo", [P, 2 * WN], F32R)
        x = [sb(f"x{u}", [P, D]) for u in range(4)]
        xT_hi = [sb(f"xT_hi{u}", [P, D], F32R) for u in range(2)]
        xT_lo = [sb(f"xT_lo{u}", [P, D], F32R) for u in range(2)]
        act_g = [sb(f"act_g{u}", [P, I]) for u in range(2)]
        h = [sb(f"h{u}", [P, I]) for u in range(2)]
        hT_hi = [sb(f"hT_hi{u}", [P, I], F32R) for u in range(2)]
        hT_lo = [sb(f"hT_lo{u}", [P, I], F32R) for u in range(2)]
        o = [sb(f"o{u}", [P, D]) for u in range(4)]
        psX = ps("psX", [P, 512])
        psG = ps("psG", [P, I])
        psU = ps("psU", [P, I])
        psH = ps("psH", [P, I])
        psO = [ps(f"psO{u}", [P, 512]) for u in range(2)]

        raw_in = [sem(f"raw_in{v}") for v in range(2)]
        split_ok = sem("split_ok")
        pool_passed = sem("pool_passed")
        hi_w_ok = sem("hi_w_ok")
        x_in = [sem(f"x_in{u}") for u in range(4)]
        x_t = sem("x_t")
        xhi_ok = sem("xhi_ok")
        xlo_ok = sem("xlo_ok")
        g_ps = sem("g_ps")
        gu_ps = sem("gu_ps")
        act_ok = sem("act_ok")
        h_ok = sem("h_ok")
        h_t = sem("h_t")
        hhi_ok = sem("hhi_ok")
        hlo_ok = sem("hlo_ok")
        o_ps = sem("o_ps")
        o_ok = sem("o_ok")
        o_out = [sem(f"o_out{u}") for u in range(4)]

        x_v = grouped_d.rearrange("(t p) d -> t p d", p=P)
        o_v = routed_d.rearrange("(t p) d -> t p d", p=P)
        NIT = NRT // 4

        with nc.Block() as block:
            @block.sync
            def _(sp):
                def load(t, u):
                    sp.dma_start(x[u][:], x_v[ds(t, 1)].rearrange("o p d -> (o p) d")).then_inc(x_in[u], 16)

                def store(t, u):
                    sp.wait_ge(o_ok, t + 1)
                    sp.dma_start(o_v[ds(t, 1)].rearrange("o p d -> (o p) d"), o[u][:]).then_inc(o_out[u], 16)

                for u in range(4):
                    load(u, u)
                with sp.Fori(0, NIT - 1) as i:
                    for u in range(4):
                        sp.wait_ge(x_t, 4 * i + u + 1)
                        load(4 * i + 4 + u, u)
                        store(4 * i + u, u)
                for u in range(4):
                    store(NRT - 4 + u, u)
                for u in range(4):
                    sp.wait_ge(o_out[u], 16 * NIT)

            @block.gpsimd
            def _(pool):
                def load(e, v):
                    for w, at, k in ((gate_w, WG, KD), (up_w, WU, KD), (down_w, WD, KI)):
                        n = w.shape[2]
                        pool.dma_start(raw[v][:, at:at + k * n].rearrange("p (k n) -> p k n", k=k),
                                       w[ds(e, 1)].rearrange("o (k p) n -> p (o k) n", p=P)).then_inc(raw_in[v], 16)

                def split(e, v, j, wait_tiles):
                    pool.wait_ge(raw_in[v], 48 * j + 48)
                    if wait_tiles:
                        ended = pool.value_load(expert_end[0:1, ds(e - 2, 1)], min_val=1, max_val=NRT + 1)
                        pool.wait_ge(o_ps, ended)
                        hold(pool, pool_passed)
                    hi = w_hi[:, v * WN:(v + 1) * WN]
                    pool.tensor_scalar(hi, raw[v][:], 1.0, 0.0, ALU.mult, ALU.add).then_inc(hi_w_ok, 1)
                    pool.wait_ge(hi_w_ok, e + 1)
                    pool.tensor_tensor(w_lo[:, v * WN:(v + 1) * WN], raw[v][:], hi.bitcast(F32), ALU.subtract).then_inc(split_ok, 1)

                pool.sem_inc(o_ps, 1)
                load(0, 0)
                load(1, 1)
                for v in range(2):
                    split(v, v, 0, False)
                    pool.wait_ge(split_ok, v + 1)
                    load(2 + v, v)
                with pool.Fori(1, E // 2 - 1) as j:
                    for v in range(2):
                        split(2 * j + v, v, j, True)
                        pool.wait_ge(split_ok, 2 * j + v + 1)
                        load(2 * j + 2 + v, v)
                for v in range(2):
                    split(E - 2 + v, v, E // 2 - 1, True)

            @block.scalar
            def _(act):
                def x_hi(t, u):
                    act.wait_ge(x_t, t + 1)
                    if positive(t - 1):
                        act.wait_ge(gu_ps, t - 1)
                    act.copy(xT_hi[u % 2][:], psX[:, 0:D]).then_inc(xhi_ok, 1)

                def gate(t, u):
                    act.wait_ge(g_ps, t + 1)
                    if positive(t - 1):
                        act.wait_ge(h_ok, t - 1)
                    act.activation(act_g[u % 2][:], psG[:], ACT.Silu).then_inc(act_ok, 1)

                def h_hi(t, u):
                    act.wait_ge(h_t, t + 1)
                    if positive(t - 1):
                        act.wait_ge(o_ps, t)
                    act.copy(hT_hi[u % 2][:], psH[:]).then_inc(hhi_ok, 1)

                def half(t, u, i):
                    act.wait_ge(o_ps, t + 2)
                    if positive(i):
                        act.wait_ge(o_out[u], 16 * i)
                    act.mul(o[u][:], psO[u % 2][:, 0:D], 0.5).then_inc(o_ok, 1)

                def tile(t, u, i):
                    if positive(t):
                        h_hi(t - 1, (u - 1) % 4)
                    gate(t, u)
                    if not isinstance(t, int) or t + 1 < NRT:
                        x_hi(t + 1, (u + 1) % 4)
                    if positive(t):
                        half(t - 1, (u - 1) % 4, i - 1 if u == 0 else i)

                x_hi(0, 0)
                for u in range(4):
                    tile(u, u, 0)
                with act.Fori(1, NIT - 1) as i:
                    for u in range(4):
                        tile(4 * i + u, u, i)
                for u in range(4):
                    tile(NRT - 4 + u, u, NIT - 1)
                h_hi(NRT - 1, 3)
                half(NRT - 1, 3, NIT - 1)

            @block.vector
            def _(dve):
                def x_lo(t, u):
                    dve.wait_ge(xhi_ok, t + 1)
                    dve.tensor_tensor(xT_lo[u % 2][:], psX[:, 0:D], xT_hi[u % 2][:].bitcast(F32), ALU.subtract).then_inc(xlo_ok, 1)

                def mul(t, u):
                    dve.wait_ge(act_ok, t + 1)
                    dve.wait_ge(gu_ps, t + 1)
                    if positive(t - 1):
                        dve.wait_ge(h_t, t - 1)
                    dve.tensor_tensor(h[u % 2][:], act_g[u % 2][:], psU[:], ALU.mult).then_inc(h_ok, 1)

                def h_lo(t, u):
                    dve.wait_ge(hhi_ok, t + 1)
                    dve.tensor_tensor(hT_lo[u % 2][:], psH[:], hT_hi[u % 2][:].bitcast(F32), ALU.subtract).then_inc(hlo_ok, 1)

                def tile(t, u):
                    if positive(t):
                        h_lo(t - 1, (u - 1) % 4)
                    mul(t, u)
                    if not isinstance(t, int) or t + 1 < NRT:
                        x_lo(t + 1, (u + 1) % 4)

                x_lo(0, 0)
                for u in range(4):
                    tile(u, u)
                with dve.Fori(1, NIT - 1) as i:
                    for u in range(4):
                        tile(4 * i + u, u)
                for u in range(4):
                    tile(NRT - 4 + u, u)
                h_lo(NRT - 1, 3)

            @block.tensor
            def _(pe):
                def turn_x(t, u, i):
                    pe.wait_ge(x_in[u], 16 * i + 16)
                    if positive(t):
                        pe.wait_ge(xlo_ok, t)
                    for k in range(KD):
                        last = pe.transpose(psX[:, k * P:(k + 1) * P], x[u][:, k * P:(k + 1) * P], ident[:])
                    last.then_inc(x_t, 1)

                def gate_up(t, u, slot):
                    pe.wait_ge(xlo_ok, t + 1)
                    if positive(t):
                        pe.wait_ge(h_ok, t)
                    for at, dst, done in ((WG, psG, g_ps), (WU, psU, gu_ps)):
                        g = 0
                        for k in range(KD):
                            for xT, w in ((xT_hi, w_hi), (xT_lo, w_hi), (xT_hi, w_lo)):
                                last = pe.matmul(dst[:], xT[u % 2][:, k * P:(k + 1) * P], w[:, ds(slot * WN + (at + k * I), I)],
                                                 start=(g == 0), stop=(g == 3 * KD - 1))
                                g += 1
                        last.then_inc(done, 1)

                def turn_h(t, u):
                    pe.wait_ge(h_ok, t + 1)
                    if positive(t):
                        pe.wait_ge(hlo_ok, t)
                    for k in range(KI):
                        last = pe.transpose(psH[:, k * P:(k + 1) * P], h[u % 2][:, k * P:(k + 1) * P], ident[:])
                    last.then_inc(h_t, 1)

                def down(t, u, slot):
                    pe.wait_ge(hlo_ok, t + 1)
                    if positive(t - 1):
                        pe.wait_ge(o_ok, t - 1)
                    g = 0
                    for k in range(KI):
                        for hT, w in ((hT_hi, w_hi), (hT_lo, w_hi), (hT_hi, w_lo)):
                            last = pe.matmul(psO[u % 2][:, 0:D], hT[u % 2][:, k * P:(k + 1) * P], w[:, ds(slot * WN + (WD + k * D), D)],
                                             start=(g == 0), stop=(g == 3 * KI - 1))
                            g += 1
                    last.then_inc(o_ps, 1)

                def expert_of(t):
                    return pe.value_load(tile_expert[0:1, ds(t, 1)], min_val=0, max_val=E - 1)

                def slot_of(e):
                    return pe.snap(e % 2, min_val=0, max_val=1)

                def tile(t, u, i):
                    e = expert_of(t)
                    slot = slot_of(e)
                    if positive(t):
                        slot_before = slot_of(expert_of(t - 1))
                        turn_h(t - 1, (u - 1) % 4)
                    pe.wait_ge(split_ok, e + 1)
                    gate_up(t, u, slot)
                    if not isinstance(t, int) or t + 1 < NRT:
                        turn_x(t + 1, (u + 1) % 4, i + 1 if u == 3 else i)
                    if positive(t):
                        down(t - 1, (u - 1) % 4, slot_before)

                turn_x(0, 0, 0)
                for u in range(4):
                    tile(u, u, 0)
                with pe.Fori(1, NIT - 1) as i:
                    for u in range(4):
                        tile(4 * i + u, u, i)
                for u in range(4):
                    tile(NRT - 4 + u, u, NIT - 1)
                turn_h(NRT - 1, 3)
                down(NRT - 1, 3, slot_of(expert_of(NRT - 1)))


def attention(nc, s, y_d, routed_d, out_d, stack_d, w_inT, b_in, w_outT, b_out, place, ident):
    with ExitStack() as ctx:
        taken = semaphores(nc, ctx)

        def sb(name, shape, dt=F32):
            return ctx.enter_context(nc.sbuf_tensor(f"at_{name}", shape, dt))

        def ps(name, shape):
            return ctx.enter_context(nc.psum_tensor(f"at_{name}", shape, F32))

        def sem(name):
            return taken(f"at_{name}")

        J, KD, D, B, T, H, HD = s.J, s.KD, s.D, s.B, s.T, s.H, s.HD
        STEPS, QUAD = 16, 4
        HG = P // HD
        VW = P + HD
        SCALE = float(HD) ** -0.5

        def keys(qt):
            return list(range(max(0, qt - 1), min(J - 1, qt + 1) + 1))

        def units(st):
            return len(keys(st // 4))

        UNITS = sum(units(st) for st in range(STEPS))
        unit_at = [sum(units(x) for x in range(st)) for st in range(STEPS + 1)]

        def by_act(n):
            return n == 2
        act_at = [sum(by_act(n) for x in range(st) for n in range(units(x))) for st in range(STEPS + 1)]
        dve_at = [unit_at[st] - act_at[st] for st in range(STEPS + 1)]

        w_hi = sb("w_hi", [P, KD, 3 * D], F32R)
        w_lo = sb("w_lo", [P, KD, 3 * D], F32R)
        wo_hi = sb("wo_hi", [P, KD, D], F32R)
        wo_lo = sb("wo_lo", [P, KD, D], F32R)
        bqk = sb("bqk", [P, 4])
        bv = sb("bv", [P, D])
        bo = sb("bo", [P, D])
        ident_bf = sb("ident_bf", [P, P], BF16)
        mask = sb("mask", [P, 2, P], BF16)

        with (
            nc.sbuf_tensor("at_w_raw", [P, KD, 3 * D], F32) as w_raw,
            nc.sbuf_tensor("at_wo_raw", [P, KD, D], F32) as wo_raw,
            nc.sbuf_tensor("at_bqk_raw", [P, 4], F32) as bqk_raw,
            nc.Block() as block,
        ):
            in_ = sem("w_in")
            pre = sem("pre")
            chain = sem("w_chain")

            @block.sync
            def _(sp):
                sp.dma_start(w_raw[:], w_inT.rearrange("(k p) n -> p k n", p=P)).then_inc(in_, 16)
                sp.dma_start(wo_raw[:], w_outT.rearrange("(k p) n -> p k n", p=P)).then_inc(in_, 16)
                for n, at in enumerate((0, D, P, D + P)):
                    sp.dma_start(bqk_raw[:, n:n + 1], b_in[at:at + P].rearrange("(p o) -> p o", o=1)).then_inc(in_, 16)
                sp.dma_start(bv[:], b_in[2 * D:3 * D].rearrange("(o n) -> o n", o=1).broadcast_to([P, D])).then_inc(in_, 16)
                sp.dma_start(bo[:], b_out.rearrange("(o n) -> o n", o=1).broadcast_to([P, D])).then_inc(in_, 16)
                sp.wait_ge(in_, 16 * 8)

            @block.gpsimd
            def _(pool):
                pool.memset(ident_bf[:], 0.0).then_inc(pre, 1)
                pool.memset(mask[:], 0.0).then_inc(pre, 1)
                pool.wait_ge(pre, 2)
                pool.affine_select(out=ident_bf[:], in_=ident_bf[:], compare_op=ALU.not_equal, fill=1.0, base=0,
                                   pattern=[[-1, P]], channel_multiplier=1)
                pool.affine_select(out=mask[:, 0, :], in_=mask[:, 0, :], compare_op=ALU.is_ge, fill=NEG, base=P - WINDOW,
                                   pattern=[[1, P]], channel_multiplier=-1)
                pool.affine_select(out=mask[:, 1, :], in_=mask[:, 1, :], compare_op=ALU.is_ge, fill=NEG, base=WINDOW - P,
                                   pattern=[[-1, P]], channel_multiplier=1)

            @block.vector
            def _(dve):
                dve.wait_ge(in_, 16 * 8)
                dve.tensor_scalar(w_raw[:, :, 0:D], w_raw[:, :, 0:D], SCALE, None, ALU.mult).then_inc(chain, 1)
                dve.wait_ge(chain, 1)
                dve.tensor_copy(w_hi[:], w_raw[:]).then_inc(chain, 1)
                dve.tensor_copy(wo_hi[:], wo_raw[:]).then_inc(chain, 1)
                dve.tensor_copy(bqk[:], bqk_raw[:]).then_inc(chain, 1)
                dve.wait_ge(chain, 4)
                dve.tensor_tensor(w_lo[:], w_raw[:], w_hi[:].bitcast(F32), ALU.subtract)
                dve.tensor_tensor(wo_lo[:], wo_raw[:], wo_hi[:].bitcast(F32), ALU.subtract)
                for n in (0, 2):
                    dve.tensor_scalar(bqk[:, n:n + 1], bqk_raw[:, n:n + 1], SCALE, None, ALU.mult)

        q_st = sb("q_st", [P, H, T], F32R)
        k_st = [sb(f"k_st{v}", [P, H // 2, T], F32R) for v in range(2)]
        v_dg = sb("v_dg", [P, J, 2, HG * VW])
        prob = [sb(f"prob{v}", [P, QUAD, 3 * P]) for v in range(2)]
        probT = [sb(f"probT{v}", [P, 12 * P]) for v in range(2)]
        xT_hi = sb("xT_hi", [P, KD, T], F32R)
        xT_lo = sb("xT_lo", [P, KD, T], F32R)
        pr_hi = [sb(f"pr_hi{v}", [P, T], F32R) for v in range(2)]
        pr_lo = [sb(f"pr_lo{v}", [P, T], F32R) for v in range(2)]
        x = sb("x", [P, J, D])
        r = sb("r", [P, J, D])
        xn = sb("xn", [P, J, D])
        res = [sb(f"res{v}", [P, J, D]) for v in range(2)]
        o = sb("o", [P, J, D])
        place_c = sb("place_c", [P, J], I32)
        stats = sb("stats", [P, J, 6])
        mv = sb("mv", [P, J, 2])
        vare = sb("vare", [P, J])
        rstd = sb("rstd", [P, J])
        neg_half = sb("neg_half", [P, J])
        nmax = [sb(f"nmax{v}", [P, QUAD]) for v in range(2)]
        total = [sb(f"total{v}", [P, H]) for v in range(2)]
        inv = sb("inv", [P, H])
        inv_w = sb("inv_w", [P, D])
        invT = sb("invT", [P, D])
        ctxt = sb("ctxt", [P, D])
        ctx_hi = sb("ctx_hi", [P, D], F32R)
        ctx_lo = sb("ctx_lo", [P, D], F32R)

        psS = [ps(f"psS{v}", [P, 2, 512]) for v in range(2)]
        psT = [ps(f"psT{v}", [P, 512]) for v in range(2)]
        psC = ps("psC", [P, 512])
        psM = ps("psM", [P, 512])

        s_ps = sem("s_ps")
        mx_ok = sem("mx_ok")
        ex_ok = sem("ex_ok")
        t_ps = sem("t_ps")
        pta_ok = sem("pta_ok")
        ptv_ok = sem("ptv_ok")
        pv_ok = sem("pv_ok")
        inv_ok = sem("inv_ok")
        invw_ok = sem("invw_ok")
        i_ps = sem("i_ps")
        invT_ok = sem("invT_ok")
        c_ok = sem("c_ok")
        chi_ok = sem("chi_ok")
        clo_ok = sem("clo_ok")
        o_ps = sem("o_ps")
        o_ok = sem("o_ok")
        o_out = sem("o_out")
        y_in = sem("y_in")
        r_in = sem("r_in")
        place_ok = sem("place_ok")
        x_ok = sem("x_ok")
        stat_ok = sem("stat_ok")
        vare_ok = sem("vare_ok")
        rstd_ok = sem("rstd_ok")
        xn_ok = sem("xn_ok")
        sum_ok = sem("sum_ok")
        res_ok = sem("res_ok")
        x_ps = sem("x_ps")
        xhi_ok = sem("xhi_ok")
        xlo_ok = sem("xlo_ok")
        p_ps = sem("p_ps")
        phi_ok = sem("phi_ok")
        plo_ok = sem("plo_ok")
        spill = [sem(f"spill{n}") for n in range(4)]
        stacked = [sem(f"stacked{n}") for n in range(4)]
        q_late = [sem(f"q_late{m}") for m in range(2)]
        v_ps = sem("v_ps")
        v_ok = sem("v_ok")
        dve_passed = sem("dve_passed")
        pool_passed = sem("pool_passed")
        zero_ok = sem("zero_ok")

        def view(d):
            return d.rearrange("(c j p) d -> c p j d", j=J, p=P)

        def batch(v, b):
            return v[ds(b, 1)].rearrange("o p j d -> (o p) j d")

        y_v, out_v = view(y_d), view(out_d)

        A_JOBS = {2: ("v", 2, 0), 3: ("v", 3, 0), 4: ("x", 0, 1), 5: ("x", 1, 1), 6: ("p", 0, 1), 7: ("p", 1, 1),
                  8: ("p", 2, 1), 9: ("p", 3, 1), 10: ("v", 0, 1), 13: ("v", 1, 1)}
        B_JOBS = {st: ("i", st // 4 - 1, 0) for st in range(0, 16, 4)} | {st: ("o", st // 4 - 1, 0) for st in range(1, 16, 4)}

        def jobs(b, first, last):
            found = []
            for st in range(STEPS):
                if st in A_JOBS:
                    kind, n, ahead = A_JOBS[st]
                    if not (ahead and last):
                        found.append((st, "a", kind, n, b + ahead))
                if st in B_JOBS:
                    kind, n, _ = B_JOBS[st]
                    if n >= 0:
                        found.append((st, "b", kind, n, b))
                    elif not first:
                        found.append((st, "b", kind, J - 1, b - 1))
            return found

        def job_done(kind, n, b):
            return {"v": (v_ok, J * b + n + 1), "x": (xlo_ok, KD * b + n + 1), "p": (plo_ok, 4 * b + n + 1),
                    "i": (invT_ok, J * b + n + 1), "o": (o_ok, J * b + n + 1)}[kind]

        AHEAD = [("x", 0), ("x", 1), ("p", 0), ("p", 1), ("p", 2), ("p", 3), ("v", 0), ("v", 1)]

        def each_batch(eng, body):
            body(0, 0, True, False)
            body(1, 1, False, False)
            with eng.Fori(1, B // 2 - 1) as i:
                for v in range(2):
                    body(2 * i + v, v, False, False)
            body(B - 2, 0, False, False)
            body(B - 1, 1, False, True)

        with nc.Block() as block:
            @block.sync
            def _(sp):
                def load(b):
                    sp.dma_start(x[:], batch(y_v, b)).then_inc(y_in, 16)

                def stack(n, b, v):
                    side, m = n % 2, n // 2
                    read, spilled, scored = (ahead_of_wait(sp, value) for value in (96 * b, 32 * b + 32, 2 * STEPS * b - STEPS))
                    sp.wait_ge(plo_ok, 4 * b + n + 1)
                    if positive(b):
                        sp.wait_ge(stacked[n], read)
                        if side == 0:
                            sp.wait_ge(q_late[m], read)
                    rows = slice(m * P, (m + 1) * P)
                    sp.dma_start(stack_d[side, 0, rows, :], pr_hi[n % 2][:].bitcast(F32)).then_inc(spill[n], 16)
                    sp.dma_start(stack_d[side, 1, rows, :], pr_lo[n % 2][:].bitcast(F32)).then_inc(spill[n], 16)
                    sp.wait_ge(spill[n], spilled)
                    if side == 0:
                        if positive(2 * STEPS * b):
                            sp.wait_ge(s_ps, scored)
                        q_rows(m, 0, stacked[n])
                        return
                    for at_row, part in enumerate((0, 1, 0)):
                        src = stack_d[1, part, rows, :].rearrange("(h e d) t -> e d h t", e=2, d=HD)
                        for e in range(2):
                            at = 64 * e + HD * at_row
                            dst = k_st[v][at:at + HD, m * HG // 2:(m + 1) * HG // 2, :]
                            sp.dma_start(dst.bitcast(F32), src[e]).then_inc(stacked[n], 16)

                def q_rows(m, half, landed):
                    ts = slice(half * T // 2, (half + 1) * T // 2)
                    for at_row, part in enumerate((0, 0, 1)):
                        src = stack_d[0, part, m * P:(m + 1) * P, ts].rearrange("(h e d) t -> e d h t", e=2, d=HD)
                        for e in range(2):
                            at = 64 * e + HD * at_row
                            dst = q_st[at:at + HD, m * HG + e:(m + 1) * HG:2, ts]
                            sp.dma_start(dst.bitcast(F32), src[e]).then_inc(landed, 16)

                def q_second(b):
                    if positive(2 * STEPS * b):
                        sp.wait_ge(s_ps, 2 * STEPS * b)
                    for m in range(2):
                        q_rows(m, 1, q_late[m])

                def store(b):
                    sp.wait_ge(o_ok, J * b + J)
                    sp.dma_start(batch(out_v, b), o[:]).then_inc(o_out, 16)

                def body(b, v, first, last):
                    q_second(b)
                    if not first:
                        store(b - 1)
                    if not last:
                        if not (isinstance(b, int) and b + 2 >= B):
                            sp.wait_ge(sum_ok, b + 2)
                            load(b + 2)
                        for n in range(4):
                            stack(n, b + 1, 1 - v)

                load(0)
                sp.wait_ge(zero_ok, 5)
                for n in range(4):
                    stack(n, 0, 0)
                sp.wait_ge(sum_ok, 1)
                load(1)
                each_batch(sp, body)
                store(B - 1)
                sp.wait_ge(o_out, 16 * B)

            @block.gpsimd
            def _(pool):
                def gather(b):
                    pool.tensor_copy(place_c[:], place[:, ds(b * J, J)]).then_inc(place_ok, 1)
                    pool.wait_ge(place_ok, b + 1)
                    hold(pool, pool_passed)
                    for j in range(J):
                        pool.indirect_dma_start(out=r[:, j, :], out_offset=None, in_=routed_d,
                                                in_offset=bass.IndirectOffsetOnAxis(ap=place_c[:, j:j + 1], axis=0)
                                                ).then_inc(r_in, 16)

                def ahead(b, v, more):
                    pool.wait_ge(y_in, 16 * b + 16)
                    pool.wait_ge(r_in, 16 * J * b + 16 * J)
                    pool.tensor_tensor(x[:], x[:], r[:], ALU.add).then_inc(x_ok, 1)
                    pool.wait_ge(x_ok, b + 1)
                    if more:
                        gather(b + 1)
                    pool.wait_ge(vare_ok, b + 1)
                    pool.tensor_tensor(rstd[:], vare[:], neg_half[:], ALU.pow).then_inc(rstd_ok, 1)
                    pool.wait_ge(xn_ok, b + 1)
                    if positive(J * b - J):
                        pool.wait_ge(o_ok, J * b - J)
                    pool.tensor_tensor(res[v][:], x[:], xn[:], ALU.add).then_inc(sum_ok, 1)
                    pool.wait_ge(sum_ok, b + 1)
                    pool.tensor_tensor(res[v][:], res[v][:], bo[:].unsqueeze(1).broadcast_to([P, J, D]), ALU.add).then_inc(res_ok, 1)

                pool.memset(neg_half[:], -0.5).then_inc(zero_ok, 1)
                pool.memset(k_st[0][:].bitcast(F32), 0.0).then_inc(zero_ok, 1)
                pool.memset(k_st[1][:].bitcast(F32), 0.0).then_inc(zero_ok, 1)
                pool.wait_ge(zero_ok, 5)
                gather(0)
                ahead(0, 0, True)

                def body(b, v, first, last):
                    if not last:
                        ahead(b + 1, 1 - v, not (isinstance(b, int) and b + 2 >= B))

                each_batch(pool, body)

            @block.scalar
            def _(act):
                def job(kind, n, b):
                    if kind == "x":
                        act.wait_ge(x_ps, KD * b + n + 1)
                        if n == 0 and positive(J * b):
                            act.wait_ge(v_ps, J * b)
                        act.copy(xT_hi[:, n, :], psM[:]).then_inc(xhi_ok, 1)
                    elif kind == "p":
                        act.wait_ge(p_ps, 4 * b + n + 1)
                        if n >= 2:
                            act.wait_ge(spill[n - 2], 32 * b + 32)
                        elif positive(b):
                            act.wait_ge(spill[n + 2], 32 * b)
                        act.activation(pr_hi[n % 2][:], psM[:], ACT.Identity, bias=bqk[:, n:n + 1]).then_inc(phi_ok, 1)
                    elif kind == "i":
                        act.wait_ge(i_ps, J * b + n + 1)
                        if positive(J * b + n):
                            act.wait_ge(c_ok, J * b + n)
                        act.copy(invT[:], psM[:, 0:D]).then_inc(invT_ok, 1)

                def context_hi(n, b):
                    act.wait_ge(c_ok, J * b + n + 1)
                    if positive(J * b + n):
                        act.wait_ge(o_ps, J * b + n)
                    act.copy(ctx_hi[:], ctxt[:]).then_inc(chi_ok, 1)

                def exps(b, st, pairs=(0, 1)):
                    v, qt = st % 2, st // 4
                    w = len(keys(qt)) * P
                    for pr in pairs:
                        act.wait_ge(mx_ok, 2 * STEPS * b + 2 * st + pr + 1)
                        if positive(STEPS * b + st - 1) and pr == 0:
                            act.wait_ge(t_ps, UNITS * b + unit_at[st] - units(st - 1))
                        if st % 4 == 0 and pr == 0 and positive(J * b + qt - 1):
                            act.wait_ge(inv_ok, J * b + qt - 1)
                        for h in range(2 * pr, 2 * pr + 2):
                            head = QUAD * (st % 4) + h
                            last = act.activation(prob[v][:, h, 0:w], psS[pr][:, h % 2, 0:w], ACT.Exp, bias=nmax[v][:, h:h + 1],
                                                  accum_out=total[qt % 2][:, head:head + 1])
                        last.then_inc(ex_ok, 1)

                def copy_out(b, st):
                    for n in range(units(st)):
                        if by_act(n):
                            act.wait_ge(t_ps, UNITS * b + unit_at[st] + n + 1)
                            if positive(STEPS * b + st - 1):
                                act.wait_ge(pv_ok, STEPS * b + st - 1)
                            act.copy(probT[st % 2][:, n * 512:(n + 1) * 512], psT[(unit_at[st] + n) % 2][:]).then_inc(pta_ok, 1)

                def body(b, v, first, last):
                    todo = jobs(b, first, last)
                    for st in range(STEPS):
                        for st_, where, kind, n, bb in todo:
                            if (st_, where) == (st - 1, "b"):
                                job(kind, n, bb)
                        ahead = (b, st + 1) if st + 1 < STEPS else (b + 1, 0)
                        if st + 1 < STEPS or not last:
                            exps(*ahead, pairs=(0,))
                        for st_, where, kind, n, bb in todo:
                            if (st_, where) == (st, "a"):
                                job(kind, n, bb)
                            if (st_, where, kind) == (st - 1, "b", "i"):
                                context_hi(n, bb)
                        if st + 1 < STEPS or not last:
                            exps(*ahead, pairs=(1,))
                        copy_out(b, st)

                for kind, n in AHEAD:
                    job(kind, n, 0)
                act.wait_ge(zero_ok, 5)
                exps(0, 0)
                each_batch(act, body)
                job("i", J - 1, B - 1)
                context_hi(J - 1, B - 1)

            @block.vector
            def _(dve):
                def norm(b, v):
                    dve.wait_ge(x_ok, b + 1)
                    for j in range(J):
                        last = dve.bn_stats(stats[:, j, :], x[:, j, :])
                    last.then_inc(stat_ok, 1)
                    dve.wait_ge(stat_ok, 2 * b + 1)
                    hold(dve, dve_passed)
                    for j in range(J):
                        last = dve.bn_aggr(mv[:, j, :], stats[:, j, :])
                    last.then_inc(stat_ok, 1)
                    dve.wait_ge(stat_ok, 2 * b + 2)
                    dve.tensor_scalar(vare[:], mv[:, :, 1], EPS, None, ALU.add).then_inc(vare_ok, 1)

                def scale(b, v):
                    dve.wait_ge(rstd_ok, b + 1)
                    if positive(KD * b):
                        dve.wait_ge(x_ps, KD * b)
                        dve.wait_ge(sum_ok, b)
                    for j in range(J):
                        last = dve.tensor_scalar(xn[:, j, :], x[:, j, :], mv[:, j, 0:1], rstd[:, j:j + 1], ALU.subtract, ALU.mult)
                    last.then_inc(xn_ok, 1)

                def job(kind, n, b, v):
                    if kind == "x":
                        dve.wait_ge(xhi_ok, KD * b + n + 1)
                        dve.tensor_tensor(xT_lo[:, n, :], psM[:], xT_hi[:, n, :].bitcast(F32), ALU.subtract).then_inc(xlo_ok, 1)
                    elif kind == "p":
                        dve.wait_ge(phi_ok, 4 * b + n + 1)
                        dve.scalar_tensor_tensor(pr_lo[n % 2][:], psM[:], bqk[:, n:n + 1], pr_hi[n % 2][:].bitcast(F32),
                                                 ALU.add, ALU.subtract).then_inc(plo_ok, 1)
                    elif kind == "v":
                        dve.wait_ge(v_ps, J * b + n + 1)
                        if positive(STEPS * b):
                            dve.wait_ge(pv_ok, STEPS * (b - 1) + 4 * min(n + 2, J))
                        dve.tensor_tensor(v_dg[:, n].rearrange("p g (h c) -> p g h c", c=VW)[:, :, :, 0:HD],
                                          psM[:, 0:D].rearrange("p (g h d) -> p g h d", g=2, d=HD),
                                          bv[:].rearrange("p (g h d) -> p g h d", g=2, d=HD), ALU.add).then_inc(v_ok, 1)
                    elif kind == "i":
                        dve.wait_ge(invT_ok, J * b + n + 1)
                        dve.wait_ge(pv_ok, STEPS * b + 4 * n + 4)
                        if positive(J * b + n):
                            dve.wait_ge(clo_ok, J * b + n)
                        dve.tensor_tensor(ctxt[:], psC[:, 0:D], invT[:], ALU.mult).then_inc(c_ok, 1)
                    elif kind == "o":
                        dve.wait_ge(o_ps, J * b + n + 1)
                        if n == 0:
                            dve.wait_ge(res_ok, b + 1)
                            if positive(b):
                                dve.wait_ge(o_out, 16 * b)
                        dve.tensor_tensor(o[:, n, :], psM[:, 0:D], res[v][:, n, :], ALU.add).then_inc(o_ok, 1)

                def context_lo(n, b):
                    dve.wait_ge(chi_ok, J * b + n + 1)
                    dve.tensor_tensor(ctx_lo[:], ctxt[:], ctx_hi[:].bitcast(F32), ALU.subtract).then_inc(clo_ok, 1)

                def maxima(b, st):
                    w = len(keys(st // 4)) * P
                    for pr in range(2):
                        dve.wait_ge(s_ps, 2 * STEPS * b + 2 * st + pr + 1)
                        if positive(2 * STEPS * b + 2 * st + pr - 3):
                            dve.wait_ge(ex_ok, 2 * STEPS * b + 2 * st + pr - 3)
                        dve.tensor_reduce(nmax[st % 2][:, 2 * pr:2 * pr + 2], psS[pr][:, :, 0:w], AX.X, ALU.max,
                                          negate=True).then_inc(mx_ok, 1)

                def copy_out(b, st):
                    for n in range(units(st)):
                        if not by_act(n):
                            dve.wait_ge(t_ps, UNITS * b + unit_at[st] + n + 1)
                            if positive(STEPS * b + st - 1):
                                dve.wait_ge(pv_ok, STEPS * b + st - 1)
                            dve.tensor_copy(probT[st % 2][:, n * 512:(n + 1) * 512], psT[(unit_at[st] + n) % 2][:]).then_inc(ptv_ok, 1)

                def invert(b, qt):
                    dve.wait_ge(ex_ok, 2 * STEPS * b + 8 * qt + 8)
                    dve.reciprocal(inv[:], total[qt % 2][:]).then_inc(inv_ok, 1)
                    dve.wait_ge(inv_ok, J * b + qt + 1)
                    if positive(J * b + qt):
                        dve.wait_ge(i_ps, J * b + qt)
                    dve.tensor_copy(inv_w[:].rearrange("p (h d) -> p h d", d=HD),
                                    inv[:].unsqueeze(2).broadcast_to([P, H, HD])).then_inc(invw_ok, 1)

                def body(b, v, first, last):
                    todo = jobs(b, first, last)
                    def jobs_at(st, place):
                        for st_, where, kind, n, bb in todo:
                            if (st_, where) == (st, place):
                                own = 1 - v if n == J - 1 and kind == "o" else v
                                job(kind, n, bb, own)

                    for st in range(STEPS):
                        jobs_at(st - 1, "b")
                        if st + 1 < STEPS:
                            maxima(b, st + 1)
                        elif not last:
                            maxima(b + 1, 0)
                        copy_out(b, st)
                        jobs_at(st, "a")
                        for st_, _, kind, n, bb in todo:
                            if (st_, kind) == (st - 1, "i"):
                                context_lo(n, bb)
                        if st == 0 and not last:
                            norm(b + 1, 1 - v)
                        if st == 1 and not last:
                            scale(b + 1, 1 - v)
                        if st % 4 == 3:
                            invert(b, st // 4)

                dve.memset(q_st[:].bitcast(F32), 0.0).then_inc(zero_ok, 1)
                dve.memset(v_dg[:], 0.0).then_inc(zero_ok, 1)
                dve.wait_ge(zero_ok, 5)
                norm(0, 0)
                scale(0, 0)
                for kind, n in AHEAD:
                    job(kind, n, 0, 0)
                maxima(0, 0)
                each_batch(dve, body)
                job("i", J - 1, B - 1, 1)
                context_lo(J - 1, B - 1)
                job("o", J - 1, B - 1, 1)

            @block.tensor
            def _(pe):
                def split3(out, pairs):
                    g = 0
                    for (a_hi, a_lo), (b_hi, b_lo) in pairs:
                        for left, right in ((a_hi, b_hi), (a_hi, b_lo), (a_lo, b_hi)):
                            last = pe.matmul(out, left, right, start=(g == 0), stop=(g == 3 * len(pairs) - 1))
                            g += 1
                    return last

                def job(kind, n, b, before):
                    if before:
                        pe.wait_ge(*job_done(*before))
                    if kind == "x":
                        pe.wait_ge(xn_ok, b + 1)
                        for j in range(J):
                            last = pe.transpose(psM[:, j * P:(j + 1) * P], xn[:, j, n * P:(n + 1) * P], ident[:])
                        last.then_inc(x_ps, 1)
                    elif kind == "p":
                        pe.wait_ge(xlo_ok, KD * b + KD)
                        at = (n % 2) * D + (n // 2) * P
                        split3(psM[:], [((w_hi[:, k, at:at + P], w_lo[:, k, at:at + P]), (xT_hi[:, k, :], xT_lo[:, k, :]))
                                        for k in range(KD)]).then_inc(p_ps, 1)
                    elif kind == "v":
                        pe.wait_ge(xlo_ok, KD * b + KD)
                        ts = slice(n * P, (n + 1) * P)
                        split3(psM[:, 0:D], [((xT_hi[:, k, ts], xT_lo[:, k, ts]), (w_hi[:, k, 2 * D:3 * D], w_lo[:, k, 2 * D:3 * D]))
                                             for k in range(KD)]).then_inc(v_ps, 1)
                    elif kind == "i":
                        pe.wait_ge(invw_ok, J * b + n + 1)
                        for k in range(KD):
                            last = pe.transpose(psM[:, k * P:(k + 1) * P], inv_w[:, k * P:(k + 1) * P], ident[:])
                        last.then_inc(i_ps, 1)
                    elif kind == "o":
                        pe.wait_ge(clo_ok, J * b + n + 1)
                        split3(psM[:, 0:D], [((ctx_hi[:, k * P:(k + 1) * P], ctx_lo[:, k * P:(k + 1) * P]),
                                              (wo_hi[:, k, :], wo_lo[:, k, :])) for k in range(KD)]).then_inc(o_ps, 1)

                def scores(b, st, v):
                    qt, w = st // 4, len(keys(st // 4)) * P
                    if st == 0:
                        for n in range(2):
                            pe.wait_ge(stacked[n], 96 * b + 96)
                    if st == 2:
                        for n in range(2, 4):
                            pe.wait_ge(stacked[n], 96 * b + 96)
                    if st in (8, 10):
                        pe.wait_ge(q_late[(st - 8) // 2], 96 * b + 96)
                    for pr in range(2):
                        if positive(2 * STEPS * b + 2 * st + pr - 1):
                            pe.wait_ge(ex_ok, 2 * STEPS * b + 2 * st + pr - 1)
                        for e in range(2):
                            head = QUAD * (st % 4) + 2 * pr + e
                            pe.matmul(psS[pr][:, e, 0:w], q_st[:, head, qt * P:(qt + 1) * P],
                                      k_st[v][:, head // 2, keys(qt)[0] * P:keys(qt)[0] * P + w], start=True, stop=False)
                            if len(keys(qt)) == 3:
                                edge = psS[pr][:, e, :].rearrange("p (a c) -> p a c", c=2 * P)[:, :, 0:P]
                                last = pe.matmul(edge, ident_bf[:], mask[:], start=False, stop=True)
                            elif qt == 0:
                                last = pe.matmul(psS[pr][:, e, P:2 * P], ident_bf[:], mask[:, 1, :], start=False, stop=True)
                            else:
                                last = pe.matmul(psS[pr][:, e, 0:P], ident_bf[:], mask[:, 0, :], start=False, stop=True)
                        last.then_inc(s_ps, 1)

                def turn(b, st, lots):
                    nk = units(st)
                    for n in lots:
                        u = unit_at[st] + n
                        before = [(x, m) for x in range(st + 1) for m in range(units(x))][u - 2] if u >= 2 else None
                        if before:
                            x, m = before
                            if by_act(m):
                                pe.wait_ge(pta_ok, act_at[STEPS] * b + act_at[x] + 1)
                            else:
                                pe.wait_ge(ptv_ok, dve_at[STEPS] * b + dve_at[x] + m + 1)
                        elif positive(b):
                            pe.wait_ge(ptv_ok, dve_at[STEPS] * b - 1 + u)
                        heads = [(4 * n + i) // nk for i in range(4)]
                        pe.wait_ge(ex_ok, 2 * STEPS * b + 2 * st + heads[-1] // 2 + 1)
                        for i, h in enumerate(heads):
                            k = (4 * n + i) % nk
                            last = pe.transpose(psT[u % 2][:, i * P:(i + 1) * P], prob[st % 2][:, h, k * P:(k + 1) * P], ident[:])
                        last.then_inc(t_ps, 1)

                def sum_v(b, st):
                    qt, nk = st // 4, units(st)
                    if act_at[st + 1]:
                        pe.wait_ge(pta_ok, act_at[STEPS] * b + act_at[st + 1])
                    pe.wait_ge(ptv_ok, dve_at[STEPS] * b + dve_at[st + 1])
                    if st % 4 == 0:
                        pe.wait_ge(v_ok, J * b + min(qt + 2, J))
                        if positive(J * b + qt):
                            pe.wait_ge(c_ok, J * b + qt)
                    g = st % 4 // 2
                    for h in range(QUAD):
                        hg = QUAD * (st % 2) + h
                        for k, kt in enumerate(keys(qt)):
                            last = pe.matmul(psC[:, g * P:(g + 1) * P], v_dg[:, kt, g, hg * P:(hg + 1) * P],
                                             probT[st % 2][:, (h * nk + k) * P:(h * nk + k + 1) * P],
                                             start=(hg == 0 and k == 0), stop=(hg == HG - 1 and k == nk - 1))
                    last.then_inc(pv_ok, 1)

                def body(b, v, first, last):
                    todo = jobs(b, first, last)
                    before = [("v", 1, b)] if first else [("v", 1, b)]
                    for st in range(STEPS):
                        if st + 1 < STEPS:
                            scores(b, st + 1, v)
                        elif not last:
                            scores(b + 1, 0, 1 - v)
                        for where in "ab":
                            for st_, where_, kind, n, bb in todo:
                                if (st_, where_) == (st, where):
                                    job(kind, n, bb, before[-1])
                                    before.append((kind, n, bb))
                            if where == "a":
                                turn(b, st, range(2))
                                if st:
                                    sum_v(b, st - 1)
                                elif not first:
                                    sum_v(b - 1, STEPS - 1)
                                turn(b, st, range(2, units(st)))

                pe.wait_ge(zero_ok, 5)
                before = None
                for kind, n in AHEAD:
                    job(kind, n, 0, before)
                    before = (kind, n, 0)
                scores(0, 0, 0)
                each_batch(pe, body)
                sum_v(B - 1, STEPS - 1)
                job("i", J - 1, B - 1, ("o", J - 2, B - 1))
                job("o", J - 1, B - 1, ("i", J - 1, B - 1))


def combine(nc, s, tag, y_d, routed_d, out_d, place):
    with ExitStack() as ctx:
        taken = semaphores(nc, ctx)

        def sb(name, shape, dt=F32):
            return ctx.enter_context(nc.sbuf_tensor(f"{tag}_{name}", shape, dt))

        def sem(name):
            return taken(f"{tag}_{name}")

        J, D = s.J, s.D
        y = [sb(f"y{u}", [P, J, D]) for u in range(2)]
        r = [sb(f"r{u}", [P, J, D]) for u in range(2)]
        o = [sb(f"o{u}", [P, J, D]) for u in range(2)]
        place_c = [sb(f"place_c{u}", [P, J], I32) for u in range(2)]

        y_in = [sem(f"y_in{u}") for u in range(2)]
        r_in = [sem(f"r_in{u}") for u in range(2)]
        place_ok = sem("place_ok")
        pool_passed = sem("pool_passed")
        o_ok = sem("o_ok")
        o_out = [sem(f"o_out{u}") for u in range(2)]

        def view(d):
            return d.rearrange("(c j p) d -> c p j d", j=J, p=P)

        def chunk(v, c):
            return v[ds(c, 1)].rearrange("o p j d -> (o p) j d")

        y_v, out_v = view(y_d), view(out_d)
        NIT = s.NCH // 2
        with nc.Block() as block:
            @block.sync
            def _(sp):
                for u in range(2):
                    sp.dma_start(y[u][:], chunk(y_v, u)).then_inc(y_in[u], 16)
                with sp.Fori(0, NIT - 1) as i:
                    for u in range(2):
                        sp.wait_ge(o_ok, 2 * i + u + 1)
                        sp.dma_start(chunk(out_v, 2 * i + u), o[u][:]).then_inc(o_out[u], 16)
                        sp.dma_start(y[u][:], chunk(y_v, 2 * i + 2 + u)).then_inc(y_in[u], 16)
                for u in range(2):
                    sp.wait_ge(o_ok, s.NCH - 1 + u)
                    sp.dma_start(chunk(out_v, s.NCH - 2 + u), o[u][:]).then_inc(o_out[u], 16)
                for u in range(2):
                    sp.wait_ge(o_out[u], 16 * NIT)

            @block.gpsimd
            def _(pool):
                def gather(c, u):
                    if positive(c - 1):
                        pool.wait_ge(o_ok, c - 1)
                    pool.tensor_copy(place_c[u][:], place[:, ds(c * J, J)]).then_inc(place_ok, 1)
                    pool.wait_ge(place_ok, c + 1)
                    hold(pool, pool_passed)
                    for j in range(J):
                        pool.indirect_dma_start(out=r[u][:, j, :], out_offset=None, in_=routed_d,
                                                in_offset=bass.IndirectOffsetOnAxis(ap=place_c[u][:, j:j + 1], axis=0)
                                                ).then_inc(r_in[u], 16)

                for u in range(2):
                    gather(u, u)
                with pool.Fori(1, NIT) as i:
                    for u in range(2):
                        gather(2 * i + u, u)

            @block.vector
            def _(dve):
                def add(c, u, i):
                    dve.wait_ge(y_in[u], 16 * i + 16)
                    dve.wait_ge(r_in[u], 16 * J * i + 16 * J)
                    if positive(i):
                        dve.wait_ge(o_out[u], 16 * i)
                    dve.tensor_tensor(o[u][:], y[u][:], r[u][:], ALU.add).then_inc(o_ok, 1)

                for u in range(2):
                    add(u, u, 0)
                with dve.Fori(1, NIT) as i:
                    for u in range(2):
                        add(2 * i + u, u, i)


def constants(nc, ident, ones_bf, upper_bf, zeros):
    with nc.Block() as block:
        clear = nc.alloc_semaphore("const_clear")
        made = nc.alloc_semaphore("const_made")
        cleared = nc.alloc_semaphore("const_cleared")

        @block.gpsimd
        def _(pool):
            pool.memset(ident[:], 0.0).then_inc(clear, 1)
            pool.memset(ones_bf[:], 1.0).then_inc(clear, 1)
            pool.wait_ge(clear, 2)
            pool.affine_select(out=ident[:], in_=ident[:], compare_op=ALU.not_equal, fill=1.0, base=0,
                               pattern=[[-1, P]], channel_multiplier=1).then_inc(made, 1)
            pool.affine_select(out=upper_bf[:], in_=ones_bf[:], compare_op=ALU.is_gt, fill=0.0, base=0,
                               pattern=[[1, P]], channel_multiplier=-1).then_inc(made, 1)
            pool.wait_ge(made, 2)

        @block.vector
        def _(dve):
            dve.memset(zeros[:], 0.0).then_inc(cleared, 1)
            dve.wait_ge(cleared, 1)


def ffn(nc, s, tag, x_d, xn_d, y_d, grouped_d, routed_d, w, place, state, filled, first):
    ident, ones_bf, upper_bf, zeros = state
    with ExitStack() as ctx:
        def sb(name, shape, dt=F32):
            return ctx.enter_context(nc.sbuf_tensor(f"{tag}_{name}", shape, dt))

        score = sb("score", [P, s.NTL])
        tile_expert = sb("tile_expert", [1, s.NRT], I32)
        expert_end = sb("expert_end", [1, s.E], I32)
        with ExitStack() as inner:
            onehot = inner.enter_context(nc.sbuf_tensor(f"{tag}_onehot", [P, s.NTL, s.E], BF16))
            top_logit = inner.enter_context(nc.sbuf_tensor(f"{tag}_top_logit", [P, s.NTL], F32))
            router(nc, s, tag + "r", x_d, xn_d, w["gate_w"], onehot, top_logit, ident,
                   (grouped_d, zeros, filled) if first else None)
            places(nc, s, tag + "p", onehot, top_logit, score, place, tile_expert, expert_end, ones_bf, upper_bf)
        shared_ffn(nc, s, tag + "s", x_d, xn_d, y_d, grouped_d, w["shared_gate_w"], w["shared_up_w"], w["shared_down_w"],
                   score, place, ident, filled)
        routed_ffn(nc, s, tag + "e", grouped_d, routed_d, w["routed_gate_w"], w["routed_up_w"], w["routed_down_w"],
                   tile_expert, expert_end, ident)


def macaron(nc, ins, out, stages=3):
    x = ins["x"].rearrange("b t d -> (b t) d")
    s = Shapes(ins["x"], ins["w_inT"], ins["gate_w"], ins["shared_gate_w"], ins["routed_gate_w"])
    out_d = out.rearrange("b t d -> (b t) d")

    def dram(name, rows):
        return nc.dram_tensor(name, [rows, s.D], F32, kind="Internal").ap()

    xn_d, y_d = dram("xn_d", s.N), dram("y_d", s.N)
    grouped_d, routed_d = dram("grouped_d", s.NRT * P), dram("routed_d", s.NRT * P)
    with (
        nc.sbuf_tensor("ident", [P, P], F32) as ident,
        nc.sbuf_tensor("ones_bf", [P, P], BF16) as ones_bf,
        nc.sbuf_tensor("upper_bf", [P, P], BF16) as upper_bf,
        nc.sbuf_tensor("place", [P, s.NTL], I32) as place,
        nc.sbuf_tensor("zeros", [P, s.D], F32) as zeros,
    ):
        constants(nc, ident, ones_bf, upper_bf, zeros)
        state = (ident, ones_bf, upper_bf, zeros)
        filled = nc.alloc_semaphore("filled")
        ffn(nc, s, "f1", x, xn_d, y_d, grouped_d, routed_d, ins, place, state, filled, True)
        if stages == 1:
            combine(nc, s, "c1", y_d, routed_d, out_d, place)
            return
        stack_d = nc.dram_tensor("stack_d", [2, 2, s.D, s.T], F32, kind="Internal").ap()
        z_d = out_d if stages == 2 else dram("z_d", s.N)
        attention(nc, s, y_d, routed_d, z_d, stack_d, ins["w_inT"], ins["b_in"], ins["w_outT"], ins["b_out"], place, ident)
        if stages == 2:
            return
        ffn(nc, s, "f2", z_d, xn_d, y_d, grouped_d, routed_d, ins, place, state, filled, False)
        combine(nc, s, "c2", y_d, routed_d, out_d, place)


_NAMES = {"x": "L0_attn_x", "w_inT": "L0_attn_w_in", "b_in": "L0_attn_b_in", "w_outT": "L0_attn_w_out", "b_out": "L0_attn_b_out",
          "gate_w": "L0_ffn_gate_w", "shared_gate_w": "L0_ffn_shared_gate_w", "shared_up_w": "L0_ffn_shared_up_w",
          "shared_down_w": "L0_ffn_shared_down_w", "routed_gate_w": "L0_ffn_routed_gate_w",
          "routed_up_w": "L0_ffn_routed_up_w", "routed_down_w": "L0_ffn_routed_down_w"}


def kernel(**inputs):
    import numpy as _np
    import concourse.bacc as _bacc
    from concourse import mybir as _mybir
    from concourse.bass_utils import run_bass_kernel_spmd as _run

    nc = _bacc.Bacc("TRN2", target_bir_lowering=False, num_devices=1)
    arrays, aps = {}, {}
    for name, given in _NAMES.items():
        a = _np.asarray(inputs[given])
        a = _np.ascontiguousarray(a.T if name.endswith("T") else a)
        arrays[f"in_{name}"] = a
        aps[name] = nc.dram_tensor(f"in_{name}", a.shape, _mybir.dt.from_np(a.dtype), kind="ExternalInput").ap()
    out = nc.dram_tensor("out_0", arrays["in_x"].shape, _mybir.dt.float32, kind="ExternalOutput").ap()
    macaron(nc, aps, out)
    r = _run(nc, [arrays], core_ids=[0])
    return r.results[0]["out_0"]
```

```python
from contextlib import ExitStack

import concourse.bass as bass
from concourse import mybir

ALU = mybir.AluOpType
ACT = mybir.ActivationFunctionType
AX = mybir.AxisListType
F32 = mybir.dt.float32
F32R = mybir.dt.float32r
BF16 = mybir.dt.bfloat16
I32 = mybir.dt.int32

P = 128
EPS = 1e-5
WINDOW = 128
NEG = -1e30
BEYOND = 1e6


class Shapes:

    def __init__(self, x, w_in, gate_w, sg, rg):
        self.B, self.T, self.D = x.shape
        self.N = self.B * self.T
        self.KD = self.D // P
        self.CH = 512
        self.J = self.CH // P
        self.NCH = self.N // self.CH
        self.NTL = self.N // P
        self.E = gate_w.shape[1]
        self.I = sg.shape[1]
        self.KI = self.I // P
        self.NRT = (self.NTL + self.E - 1 + 15) // 16 * 16
        self.PARTS = self.NCH // 2 + 4
        assert self.NRT * P % (self.PARTS * P) == 0
        self.H = 16
        self.HD = self.D // self.H


def ds(start, size):
    return bass.ds(start, size)


def positive(value):
    return not isinstance(value, int) or value > 0


def ahead_of_wait(eng, value):
    return value if isinstance(value, int) else eng.to_reg(value)


def hold(eng, passed):
    eng.sem_inc(passed, 1)


def semaphores(nc, ctx):
    held = []

    def taken(name):
        held.append(nc.alloc_semaphore(name))
        return held[-1]

    def give_back():
        nc.clear_and_free_semaphores(held)
        nc.all_engine_barrier()

    ctx.callback(give_back)
    return taken


def router(nc, s, tag, x_d, xn_d, gate_w, onehot, top_logit, ident, fill):
    with ExitStack() as ctx:
        taken = semaphores(nc, ctx)

        def sb(name, shape, dt=F32):
            return ctx.enter_context(nc.sbuf_tensor(f"{tag}_{name}", shape, dt))

        def ps(name, shape):
            return ctx.enter_context(nc.psum_tensor(f"{tag}_{name}", shape, F32))

        def sem(name):
            return taken(f"{tag}_{name}")

        J, KD, D, E = s.J, s.KD, s.D, s.E
        gw = sb("gw", [P, KD, E])
        from_e = sb("from_e", [P, E])
        neg_half = sb("neg_half", [P, J])
        x = [sb(f"x{u}", [P, J, D]) for u in range(2)]
        xn = [sb(f"xn{u}", [P, J, D]) for u in range(2)]
        xnT = [sb(f"xnT{u}", [P, KD, s.CH]) for u in range(2)]
        stats = [sb(f"stats{u}", [P, J, 6]) for u in range(2)]
        mv = [sb(f"mv{u}", [P, J, 2]) for u in range(2)]
        vare = [sb(f"vare{u}", [P, J]) for u in range(2)]
        rstd = [sb(f"rstd{u}", [P, J]) for u in range(2)]
        mx = [sb(f"mx{u}", [P, J]) for u in range(2)]
        at_top = [sb(f"at_top{u}", [P, J, E]) for u in range(2)]
        cand = [sb(f"cand{u}", [P, J, E]) for u in range(2)]
        idx = [sb(f"idx{u}", [P, J]) for u in range(2)]
        psT = [ps(f"psT{u}", [P, KD, s.CH]) for u in range(2)]
        psL = [ps(f"psL{u}", [P, 512]) for u in range(2)]

        x_in = [sem(f"x_in{u}") for u in range(2)]
        xn_out = [sem(f"xn_out{u}") for u in range(2)]
        gw_in = sem("gw_in")
        dve_passed = sem("dve_passed")
        consts = sem("consts")
        stat_ok = sem("stat_ok")
        aggr_ok = sem("aggr_ok")
        vare_ok = sem("vare_ok")
        rstd_ok = sem("rstd_ok")
        xn_ok = sem("xn_ok")
        t_ok = sem("t_ok")
        xnT_ok = sem("xnT_ok")
        lg_ps = sem("lg_ps")
        lg_ok = sem("lg_ok")
        mx_ok = sem("mx_ok")
        ix_ok = sem("ix_ok")
        idx_ok = sem("idx_ok")
        oh_ok = sem("oh_ok")

        x_v = x_d.rearrange("(c j p) d -> c p j d", j=J, p=P)
        xn_v = xn_d.rearrange("(c j p) d -> c p j d", j=J, p=P)

        with nc.Block() as block:
            @block.sync
            def _(sp):
                sp.dma_start(gw[:], gate_w.rearrange("(k p) e -> p k e", p=P)).then_inc(gw_in, 16)

                def load(c, u):
                    sp.dma_start(x[u][:], x_v[ds(c, 1)].rearrange("o p j d -> (o p) j d")).then_inc(x_in[u], 16)

                def store(c, u):
                    sp.wait_ge(xn_ok, c + 1)
                    sp.dma_start(xn_v[ds(c, 1)].rearrange("o p j d -> (o p) j d"), xn[u][:]).then_inc(xn_out[u], 16)

                def clear(i):
                    if fill:
                        rows, _, zeros, filled = fill
                        part = rows.rearrange("(g p r) d -> g p r d", g=s.PARTS, p=P)
                        sp.dma_start(part[ds(i, 1)].rearrange("o p r d -> (o p) r d"),
                                     zeros[:].unsqueeze(1).broadcast_to([P, part.shape[2], D])).then_inc(filled, 16)

                load(0, 0)
                load(1, 1)
                with sp.Fori(0, s.NCH // 2 - 1) as i:
                    for u in range(2):
                        store(2 * i + u, u)
                        load(2 * i + 2 + u, u)
                    clear(i)
                for u in range(2):
                    store(s.NCH - 2 + u, u)
                for i in range(s.NCH // 2 - 1, s.PARTS if fill else 0):
                    clear(i)
                if fill:
                    _, tail, zeros, filled = fill
                    tail = tail.rearrange("(p r) d -> p r d", p=P)
                    sp.dma_start(tail, zeros[:].unsqueeze(1).broadcast_to([P, tail.shape[1], D])).then_inc(filled, 16)
                for u in range(2):
                    sp.wait_ge(xn_out[u], 16 * (s.NCH // 2))

            @block.gpsimd
            def _(pool):
                pool.memset(neg_half[:], -0.5).then_inc(consts, 1)
                pool.iota(from_e[:], [[1, E]], base=-E, channel_multiplier=0,
                          allow_small_or_imprecise_dtypes=True).then_inc(consts, 1)
                pool.wait_ge(consts, 2)
                with pool.Fori(0, s.NCH // 2) as i:
                    for u in range(2):
                        pool.wait_ge(vare_ok, 2 * i + u + 1)
                        pool.tensor_tensor(rstd[u][:], vare[u][:], neg_half[:], ALU.pow).then_inc(rstd_ok, 1)

            @block.vector
            def _(dve):
                def norm(c, u, i):
                    dve.wait_ge(x_in[u], 16 * i + 16)
                    for j in range(J):
                        last = dve.bn_stats(stats[u][:, j, :], x[u][:, j, :])
                    last.then_inc(stat_ok, 1)
                    dve.wait_ge(stat_ok, c + 1)
                    hold(dve, dve_passed)
                    for j in range(J):
                        last = dve.bn_aggr(mv[u][:, j, :], stats[u][:, j, :])
                    last.then_inc(aggr_ok, 1)
                    dve.wait_ge(aggr_ok, c + 1)
                    dve.tensor_scalar(vare[u][:], mv[u][:, :, 1], EPS, None, ALU.add).then_inc(vare_ok, 1)

                def scale(c, u, i):
                    dve.wait_ge(rstd_ok, c + 1)
                    if positive(i):
                        dve.wait_ge(xn_out[u], 16 * i)
                        dve.wait_ge(t_ok, c - 1)
                    for j in range(J):
                        last = dve.tensor_scalar(xn[u][:, j, :], x[u][:, j, :], mv[u][:, j, 0:1], rstd[u][:, j:j + 1],
                                                 ALU.subtract, ALU.mult)
                    last.then_inc(xn_ok, 1)

                def route(c, u):
                    dve.wait_ge(lg_ps, c + 1)
                    lg = psL[u][:, 0:J * E].rearrange("p (j e) -> p j e", j=J)
                    dve.tensor_reduce(mx[u][:], lg, AX.X, ALU.max).then_inc(mx_ok, 1)
                    dve.wait_ge(mx_ok, c + 1)
                    dve.tensor_tensor(at_top[u][:], lg, mx[u][:].unsqueeze(2).broadcast_to([P, J, E]),
                                      ALU.is_equal).then_inc(lg_ok, 1)
                    dve.wait_ge(lg_ok, c + 1)
                    dve.tensor_tensor(cand[u][:], at_top[u][:], from_e[:].unsqueeze(1).broadcast_to([P, J, E]),
                                      ALU.mult).then_inc(ix_ok, 1)
                    dve.wait_ge(ix_ok, c + 1)
                    dve.tensor_reduce(idx[u][:], cand[u][:], AX.X, ALU.min).then_inc(idx_ok, 1)
                    dve.tensor_copy(top_logit[:, ds(c * J, J)], mx[u][:])
                    dve.wait_ge(idx_ok, c + 1)
                    dve.tensor_tensor(onehot[:, ds(c * J, J), :], from_e[:].unsqueeze(1).broadcast_to([P, J, E]),
                                      idx[u][:].unsqueeze(2).broadcast_to([P, J, E]), ALU.is_equal).then_inc(oh_ok, 1)

                dve.wait_ge(consts, 2)
                for c in range(4):
                    norm(c, c % 2, c // 2)
                    if c == 3:
                        route(0, 0)
                    scale(c, c % 2, c // 2)
                with dve.Fori(2, s.NCH // 2) as i:
                    for u in range(2):
                        norm(2 * i + u, u, i)
                        route(2 * i + u - 3, 1 - u)
                        scale(2 * i + u, u, i)
                for c in range(s.NCH - 3, s.NCH):
                    route(c, c % 2)
                dve.wait_ge(oh_ok, s.NCH)

            @block.scalar
            def _(act):
                def evac(c, u):
                    act.wait_ge(t_ok, c + 1)
                    if positive(c - 1):
                        act.wait_ge(lg_ps, c - 1)
                    for k in range(KD):
                        last = act.copy(xnT[u][:, k, :], psT[u][:, k, :])
                    last.then_inc(xnT_ok, 1)

                for u in range(2):
                    evac(u, u)
                with act.Fori(1, s.NCH // 2) as i:
                    for u in range(2):
                        evac(2 * i + u, u)

            @block.tensor
            def _(pe):
                def turn(c, u):
                    pe.wait_ge(xn_ok, c + 1)
                    if positive(c - 1):
                        pe.wait_ge(xnT_ok, c - 1)
                    for k in range(KD):
                        for j in range(J):
                            last = pe.transpose(psT[u][:, k, j * P:(j + 1) * P], xn[u][:, j, k * P:(k + 1) * P], ident[:])
                    last.then_inc(t_ok, 1)

                def logits(c, u):
                    pe.wait_ge(xnT_ok, c + 1)
                    if positive(c - 1):
                        pe.wait_ge(lg_ok, c - 1)
                    for j in range(J):
                        for k in range(KD):
                            last = pe.matmul(psL[u][:, j * E:(j + 1) * E], xnT[u][:, k, j * P:(j + 1) * P], gw[:, k, :],
                                             start=(k == 0), stop=(k == KD - 1))
                    last.then_inc(lg_ps, 1)

                pe.wait_ge(gw_in, 16)
                turn(0, 0)
                turn(1, 1)
                logits(0, 0)
                with pe.Fori(1, s.NCH // 2) as i:
                    turn(2 * i, 0)
                    logits(2 * i - 1, 1)
                    turn(2 * i + 1, 1)
                    logits(2 * i, 0)
                logits(s.NCH - 1, 1)


def places(nc, s, tag, onehot, top_logit, score, place, tile_run, run_expert, run_end, more_quads, ones_bf, upper_bf, ident):
    with ExitStack() as ctx:
        taken = semaphores(nc, ctx)

        def sb(name, shape, dt=F32):
            return ctx.enter_context(nc.sbuf_tensor(f"{tag}_{name}", shape, dt))

        def sem(name):
            return taken(f"{tag}_{name}")

        E, NTL = s.E, s.NTL
        G = 512 // E
        NG = NTL // G
        count = sb("count", [P, E, NTL])
        running = sb("running", [P, E * NTL + 1])
        before = running[:, 0:E * NTL].rearrange("p (e t) -> p e t", t=NTL)
        end = running[:, 1:].rearrange("p (e t) -> p e t", t=NTL)[:, :, NTL - 1]
        zero = sb("zero", [P, 1])
        n_e = sb("n_e", [P, E])
        n_i = sb("n_i", [P, E], I32)
        t_i = sb("t_i", [P, E], I32)
        t_e = sb("t_e", [P, E])
        cum = sb("cum", [P, E])
        shift = sb("shift", [P, E])
        tmp = sb("tmp", [P, E])
        row = [sb(f"row{u}", [P, G, E]) for u in range(2)]
        hit = [sb(f"hit{u}", [P, G, E]) for u in range(2)]
        place_f = sb("place_f", [P, NTL])
        tio = sb("tio", [E, s.NRT])
        one = sb("one", [E, 1])
        taken_e = sb("taken_e", [E, E])
        rank = sb("rank", [E, E])
        ends = sb("ends", [E, E])
        own = sb("own", [E, E])
        rank_c = sb("rank_c", [E, 1])
        ends_c = sb("ends_c", [E, 1])
        t_c = sb("t_c", [E, 1])
        rank_c1 = sb("rank_c1", [E, 1])
        flags = sb("flags", [E, s.NRT + 2 * E])
        late = sb("late", [1, E])
        quads_3 = sb("quads_3", [1, 1], I32)
        quads = sb("quads", [1, 1], I32)
        quads_f = sb("quads_f", [1, 1])
        spare = sb("spare", [1, 1])
        banks = [ctx.enter_context(nc.psum_tensor(f"{tag}_bank{g}", [P, G, E], F32)) for g in range(NG)]

        sums = banks[0][0:1].rearrange("p t e -> p (t e)")[:, 0:s.NRT + 2 * E]

        cnt_ps = sem("cnt_ps")
        cnt_ok = sem("cnt_ok")
        rank_ps = sem("rank_ps")
        chain = sem("chain")
        flags_ok = sem("flags_ok")
        sums_ps = sem("sums_ps")
        tio_ok = sem("tio_ok")
        score_ok = sem("score_ok")

        with nc.Block() as block:
            @block.tensor
            def _(pe):
                for g in range(NG):
                    pe.matmul(banks[g][:], ones_bf[:], onehot[:, g * G:(g + 1) * G, :], start=True,
                              stop=True).then_inc(cnt_ps, 1)
                for g in range(NG):
                    pe.wait_ge(cnt_ok, g + 1)
                    pe.matmul(banks[g][:], upper_bf[:], onehot[:, g * G:(g + 1) * G, :], start=True,
                              stop=True).then_inc(rank_ps, 1)
                pe.wait_ge(flags_ok, 1)
                pe.matmul(sums, one[:], flags[:], start=True, stop=True).then_inc(sums_ps, 1)

            @block.gpsimd
            def _(pool):
                pool.iota(tio[:], [[1, s.NRT]], base=0, channel_multiplier=0,
                          allow_small_or_imprecise_dtypes=True).then_inc(tio_ok, 1)

            @block.scalar
            def _(act):
                act.activation(score[:], top_logit[:], ACT.Sigmoid).then_inc(score_ok, 1)
                act.wait_ge(score_ok, 1)

            @block.vector
            def _(dve):
                done = [0]

                def step(ins):
                    done[0] += 1
                    ins.then_inc(chain, 1)
                    dve.wait_ge(chain, done[0])

                step(dve.memset(zero[:], 0.0))
                step(dve.memset(running[:, 0:1], 0.0))
                step(dve.memset(one[:], 1.0))
                for g in range(NG):
                    dve.wait_ge(cnt_ps, g + 1)
                    dve.tensor_copy(count[:, :, g * G:(g + 1) * G], banks[g][:].rearrange("p t e -> p e t")).then_inc(cnt_ok, 1)
                dve.wait_ge(cnt_ok, NG)
                step(dve.tensor_tensor_scan(running[:, 1:], count[:].rearrange("p e t -> p (e t)"),
                                            zero[:].broadcast_to([P, E * NTL]), 0.0, ALU.add, ALU.add))
                step(dve.tensor_copy(n_e[:, 0:1], end[:, 0:1]))
                step(dve.tensor_tensor(n_e[:, 1:E], end[:, 1:E], end[:, 0:E - 1], ALU.subtract))
                step(dve.tensor_scalar(n_i[:], n_e[:], float(P - 1), None, ALU.add))
                step(dve.tensor_scalar(t_i[:], n_i[:], 7, None, ALU.arith_shift_right))
                step(dve.tensor_copy(t_e[:], t_i[:]))
                step(dve.tensor_tensor_scan(cum[:], t_e[:], zero[:].broadcast_to([P, E]), 0.0, ALU.add, ALU.add))
                step(dve.tensor_tensor(tmp[:], cum[:], t_e[:], ALU.subtract))
                step(dve.scalar_tensor_tensor(tmp[:], tmp[:], float(P), n_e[:], ALU.mult, ALU.add))
                step(dve.tensor_tensor(shift[:], tmp[:], end, ALU.subtract))
                step(dve.tensor_tensor(count[:], before, shift[:].unsqueeze(2).broadcast_to([P, E, NTL]), ALU.add))
                for g in range(NG):
                    dve.wait_ge(rank_ps, g + 1)
                    step(dve.tensor_tensor(row[g % 2][:], banks[g][:], count[:, :, g * G:(g + 1) * G].rearrange("p e t -> p t e"), ALU.add))
                    step(dve.tensor_tensor(hit[g % 2][:], row[g % 2][:], onehot[:, g * G:(g + 1) * G, :], ALU.mult))
                    step(dve.tensor_reduce(place_f[:, g * G:(g + 1) * G], hit[g % 2][:], AX.X, ALU.add))
                step(dve.tensor_copy(place[:], place_f[:]))
                dve.wait_ge(tio_ok, 1)
                r_io = tio[:, 0:E]
                step(dve.tensor_scalar(taken_e[:], t_e[0:E, :], 1.0, None, ALU.is_ge))
                step(dve.tensor_tensor_scan(rank[:], taken_e[:], zero[0:E, :].broadcast_to([E, E]), 0.0, ALU.add, ALU.add))
                step(dve.tensor_scalar(ends[:], taken_e[:], -BEYOND, BEYOND, ALU.mult, ALU.add))
                step(dve.tensor_tensor(ends[:], ends[:], cum[0:E, :], ALU.add))
                for column, values in ((rank_c, rank[:]), (ends_c, ends[:]), (t_c, t_e[0:E, :])):
                    step(dve.tensor_tensor(own[:], values, ident[0:E, 0:E], ALU.mult))
                    step(dve.tensor_reduce(column[:], own[:], AX.X, ALU.add))
                step(dve.tensor_scalar(rank_c1[:], rank_c[:], -1.0, None, ALU.add))
                step(dve.tensor_scalar(flags[:, 0:s.NRT], tio[:], ends_c[:], None, ALU.is_ge))
                step(dve.tensor_scalar(flags[:, s.NRT:s.NRT + E], r_io, rank_c[:], None, ALU.is_ge))
                dve.tensor_scalar(flags[:, s.NRT + E:], r_io, rank_c1[:], t_c[:], ALU.is_ge, ALU.mult).then_inc(flags_ok, 1)
                step(dve.tensor_scalar(quads_3[:], cum[0:1, E - 1:E], 3.0, None, ALU.add))
                step(dve.tensor_scalar(quads[:], quads_3[:], 2, None, ALU.arith_shift_right))
                step(dve.tensor_copy(quads_f[:], quads[:]))
                step(dve.tensor_scalar(more_quads[:], quads_f[:], -float(NTL // 4), None, ALU.add))
                step(dve.scalar_tensor_tensor(spare[:], quads_f[:], 4.0, cum[0:1, E - 1:E], ALU.mult, ALU.subtract))
                step(dve.tensor_scalar(late[:], tio[0:1, 0:E], rank[0:1, E - 1:E], spare[:], ALU.is_ge, ALU.mult))
                dve.wait_ge(sums_ps, 1)
                step(dve.tensor_scalar(tile_run[:], sums[:, 0:s.NRT], float(E - 1), None, ALU.min))
                step(dve.tensor_scalar(run_expert[:], sums[:, s.NRT:s.NRT + E], float(E - 1), None, ALU.min))
                step(dve.scalar_tensor_tensor(run_end[:], sums[:, s.NRT + E:], 1.0, late[:], ALU.add, ALU.add))


def shared_ffn(nc, s, tag, x_d, xn_d, y_d, first, count, gate_w, up_w, down_w, place, ident, scatter=None, gather=None):
    with ExitStack() as ctx:
        taken = semaphores(nc, ctx)

        def sb(name, shape, dt=F32):
            return ctx.enter_context(nc.sbuf_tensor(f"{tag}_{name}", shape, dt))

        def ps(name, shape):
            return ctx.enter_context(nc.psum_tensor(f"{tag}_{name}", shape, F32))

        def sem(name):
            return taken(f"{tag}_{name}")

        J, KD, D, KI, I, CH = s.J, s.KD, s.D, s.KI, s.I, s.CH
        wg_raw = sb("wg_raw", [P, KD, I])
        wu_raw = sb("wu_raw", [P, KD, I])
        wd_raw = sb("wd_raw", [P, KI, D])
        raws = [wg_raw, wu_raw, wd_raw]
        w_hi = [sb(f"w_hi{n}", list(r.shape), F32R) for n, r in enumerate(raws)]
        w_lo = [sb(f"w_lo{n}", list(r.shape), F32R) for n, r in enumerate(raws)]
        x = [sb(f"x{u}", [P, J, D]) for u in range(2)] if scatter else None
        xn = [sb(f"xn{u}", [P, J, D]) for u in range(2)]
        GJ = J * s.NCH // count if scatter else 2 * J
        moved = [sb(f"moved{u}", [P, GJ, D]) for u in range(2)]
        source = [sb(f"source{u}", [P, GJ, D]) for u in range(2)]
        total = [sb(f"total{u}", [P, GJ, D]) for u in range(2)] if gather else None
        place_c = [sb(f"place_c{u}", [P, GJ], I32) for u in range(2)]
        y = [sb(f"y{u}", [P, J, D]) for u in range(2)]
        xT_hi = [sb(f"xT_hi{u}", [P, KD, CH], F32R) for u in range(2)]
        xT_lo = [sb(f"xT_lo{u}", [P, KD, CH], F32R) for u in range(2)]
        act_g = [sb(f"act_g{m}", [P, CH]) for m in range(2)]
        h = [sb(f"h{m}", [P, CH]) for m in range(2)]
        h_hi = [sb(f"h_hi{u}", [P, KI, CH], F32R) for u in range(2)]
        h_lo = [sb(f"h_lo{u}", [P, KI, CH], F32R) for u in range(2)]
        psT = [ps(f"psT{k}", [P, CH]) for k in range(KD)]
        psG = [ps(f"psG{m}", [P, CH]) for m in range(2)]
        psU = [ps(f"psU{m}", [P, CH]) for m in range(2)]
        psO = [ps(f"psO{m}", [P, 512]) for m in range(2)]

        w_in = sem("w_in")
        w_hi_ok = sem("w_hi_ok")
        w_ok = sem("w_ok")
        x_in = [sem(f"x_in{u}") for u in range(2)]
        xn_in = [sem(f"xn_in{u}") for u in range(2)]
        y_out = [sem(f"y_out{u}") for u in range(2)]
        source_in = [sem(f"source_in{u}") for u in range(2)]
        place_ok = sem("place_ok")
        total_ok = sem("total_ok")
        total_out = [sem(f"total_out{u}") for u in range(2)]
        pool_passed = sem("pool_passed")
        xs_ok = sem("xs_ok")
        rows_moved = [sem(f"rows_moved{u}") for u in range(2)]
        t_ok = sem("t_ok")
        hi_ok = sem("hi_ok")
        lo_ok = sem("lo_ok")
        g_ps = sem("g_ps")
        gu_ps = sem("gu_ps")
        act_ok = sem("act_ok")
        h_ok = sem("h_ok")
        hhi_ok = sem("hhi_ok")
        hlo_ok = sem("hlo_ok")
        o_ps = sem("o_ps")
        y_ok = sem("y_ok")

        def view(d):
            return d.rearrange("(c j p) d -> c p j d", j=J, p=P)

        def chunk(v, c):
            return v[ds(c, 1)].rearrange("o p j d -> (o p) j d")

        x_v, xn_v, y_v = view(x_d), view(xn_d), view(y_d)
        NIT = count // 2

        with nc.Block() as block:
            @block.sync
            def _(sp):
                for raw, w in ((wg_raw, gate_w), (wu_raw, up_w), (wd_raw, down_w)):
                    sp.dma_start(raw[:], w.rearrange("(k p) n -> p k n", p=P)).then_inc(w_in, 16)

                def load(c, u):
                    sp.dma_start(xn[u][:], chunk(xn_v, c + first)).then_inc(xn_in[u], 16)
                    if scatter:
                        sp.dma_start(x[u][:], chunk(x_v, c + first)).then_inc(x_in[u], 16)
                        group = xn_d.rearrange("(c j p) d -> c p j d", j=GJ, p=P)
                        sp.dma_start(source[u][:], chunk(group, c)).then_inc(source_in[u], 16)
                    else:
                        sp.dma_start(source[u][:, 0:J, :], chunk(x_v, c + first)).then_inc(source_in[u], 16)
                        sp.dma_start(source[u][:, J:, :], chunk(view(gather[0]), c)).then_inc(source_in[u], 16)

                def store(c, u):
                    sp.wait_ge(y_ok, J * c + J)
                    sp.dma_start(chunk(y_v, c + first), y[u][:]).then_inc(y_out[u], 16)
                    if gather:
                        sp.wait_ge(total_ok, c + 1)
                        sp.dma_start(chunk(y_v, c), total[u][:, J:, :]).then_inc(total_out[u], 16)

                load(0, 0)
                load(1, 1)
                with sp.Fori(1, NIT) as i:
                    for u in range(2):
                        store(2 * i - 2 + u, u)
                        sp.wait_ge(t_ok, 2 * i - 1 + u)
                        if scatter:
                            sp.wait_ge(xs_ok, 2 * i - 1 + u)
                        load(2 * i + u, u)
                for u in range(2):
                    store(count - 2 + u, u)
                for u in range(2):
                    sp.wait_ge(y_out[u], 16 * NIT)
                    if gather:
                        sp.wait_ge(total_out[u], 16 * NIT)

            @block.gpsimd
            def _(pool):
                def scatter_rows(c, u, i):
                    pool.wait_ge(xs_ok, c + 1)
                    pool.wait_ge(place_ok, c + 1)
                    hold(pool, pool_passed)
                    for j in range(GJ):
                        pool.indirect_dma_start(
                            out=scatter[0], out_offset=bass.IndirectOffsetOnAxis(ap=place_c[u][:, j:j + 1], axis=0),
                            in_=moved[u][:, j, :], in_offset=None).then_inc(rows_moved[u], 16)

                def scale_tokens(c, u, i):
                    pool.wait_ge(source_in[u], 16 * i + 16)
                    if positive(i):
                        pool.wait_ge(rows_moved[u], 16 * GJ * i)
                    pool.tensor_copy(place_c[u][:], place[:, ds(c * GJ, GJ)]).then_inc(place_ok, 1)
                    pool.tensor_tensor(moved[u][:], source[u][:],
                                       scatter[1][:, ds(c * GJ, GJ)].unsqueeze(2).broadcast_to([P, GJ, D]),
                                       ALU.mult).then_inc(xs_ok, 1)

                def gather_rows(c, u):
                    if positive(c - 1):
                        pool.wait_ge(total_ok, c - 1)
                    pool.tensor_copy(place_c[u][:, 0:J], place[:, ds((c + first) * J, J)]).then_inc(place_ok, 1)
                    pool.tensor_copy(place_c[u][:, J:], place[:, ds(c * J, J)]).then_inc(place_ok, 1)
                    pool.wait_ge(place_ok, 2 * c + 2)
                    hold(pool, pool_passed)
                    for j in range(GJ):
                        pool.indirect_dma_start(out=moved[u][:, j, :], out_offset=None, in_=gather[1],
                                                in_offset=bass.IndirectOffsetOnAxis(ap=place_c[u][:, j:j + 1], axis=0)
                                                ).then_inc(rows_moved[u], 16)

                def add_rows(c, u, i):
                    pool.wait_ge(source_in[u], 32 * i + 32)
                    pool.wait_ge(rows_moved[u], 16 * GJ * i + 16 * GJ)
                    if positive(i):
                        pool.wait_ge(y_ok, J * c - J)
                        pool.wait_ge(total_out[u], 16 * i)
                    pool.tensor_tensor(total[u][:], source[u][:], moved[u][:], ALU.add).then_inc(total_ok, 1)

                if scatter:
                    for u in range(2):
                        scale_tokens(u, u, 0)
                        if u == 0:
                            pool.wait_ge(scatter[2], 16 * s.PARTS + 16)
                        scatter_rows(u, u, 0)
                    with pool.Fori(1, NIT) as i:
                        for u in range(2):
                            scale_tokens(2 * i + u, u, i)
                            scatter_rows(2 * i + u, u, i)
                    for u in range(2):
                        pool.wait_ge(rows_moved[u], 16 * GJ * NIT)
                else:
                    gather_rows(0, 0)
                    gather_rows(1, 1)
                    add_rows(0, 0, 0)
                    with pool.Fori(1, NIT) as i:
                        gather_rows(2 * i, 0)
                        add_rows(2 * i - 1, 1, i - 1)
                        gather_rows(2 * i + 1, 1)
                        add_rows(2 * i, 0, i)
                    add_rows(count - 1, 1, NIT - 1)

            @block.scalar
            def _(act):
                def hi_of(c, u):
                    act.wait_ge(t_ok, c + 1)
                    if positive(KI * c - KI):
                        act.wait_ge(gu_ps, KI * c - KI)
                    for k in range(KD):
                        last = act.copy(xT_hi[u][:, k, :], psT[k][:])
                    last.then_inc(hi_ok, 1)

                def slices(c, u, last):
                    for m in range(KI):
                        act.wait_ge(g_ps, KI * c + m + 1)
                        if positive(KI * c + m - 1):
                            act.wait_ge(h_ok, KI * c + m - 1)
                        act.activation(act_g[m % 2][:], psG[m % 2][:], ACT.Silu).then_inc(act_ok, 1)
                        act.wait_ge(h_ok, KI * c + m + 1)
                        if m == 0 and positive(J * c - J):
                            act.wait_ge(o_ps, J * c - J)
                        act.copy(h_hi[u][:, m, :], h[m % 2][:]).then_inc(hhi_ok, 1)
                        if m == KI - 2 and not last:
                            hi_of(c + 1, 1 - u)

                act.wait_ge(w_in, 16 * 3)
                for n in range(3):
                    act.copy(w_hi[n][:], raws[n][:]).then_inc(w_hi_ok, 1)
                    if n == 1:
                        hi_of(0, 0)
                slices(0, 0, False)
                slices(1, 1, False)
                with act.Fori(1, NIT - 1) as i:
                    for u in range(2):
                        slices(2 * i + u, u, False)
                slices(count - 2, 0, False)
                slices(count - 1, 1, True)

            @block.vector
            def _(dve):
                def split_weight(n):
                    dve.wait_ge(w_hi_ok, n + 1)
                    dve.tensor_tensor(w_lo[n][:], raws[n][:], w_hi[n][:].bitcast(F32), ALU.subtract).then_inc(w_ok, 1)

                def lo_of(c, u):
                    dve.wait_ge(hi_ok, c + 1)
                    for k in range(KD):
                        last = dve.tensor_tensor(xT_lo[u][:, k, :], psT[k][:], xT_hi[u][:, k, :].bitcast(F32), ALU.subtract)
                    last.then_inc(lo_ok, 1)

                def add(c, j, u, i):
                    dve.wait_ge(o_ps, J * c + j + 1)
                    if j == 0:
                        if scatter:
                            dve.wait_ge(x_in[u], 16 * i + 16)
                        else:
                            dve.wait_ge(total_ok, c + 1)
                        if positive(i):
                            dve.wait_ge(y_out[u], 16 * i)
                    dve.scalar_tensor_tensor(y[u][:, j, :], psO[j % 2][:, 0:D], 0.5, (x if scatter else total)[u][:, j, :],
                                             ALU.mult, ALU.add).then_inc(y_ok, 1)

                def slices(c, u, i, last):
                    for m in range(KI):
                        dve.wait_ge(act_ok, KI * c + m + 1)
                        dve.wait_ge(gu_ps, KI * c + m + 1)
                        if positive(KI * c + m - 1):
                            dve.wait_ge(hlo_ok, KI * c + m - 1)
                        dve.tensor_tensor(h[m % 2][:], act_g[m % 2][:], psU[m % 2][:], ALU.mult).then_inc(h_ok, 1)
                        dve.wait_ge(hhi_ok, KI * c + m + 1)
                        dve.tensor_tensor(h_lo[u][:, m, :], h[m % 2][:], h_hi[u][:, m, :].bitcast(F32),
                                          ALU.subtract).then_inc(hlo_ok, 1)
                        if m == 0 and positive(c):
                            for j in range(J):
                                add(c - 1, j, 1 - u, i - 1 + u)
                        if m == KI - 2 and not last:
                            lo_of(c + 1, 1 - u)

                split_weight(0)
                split_weight(1)
                lo_of(0, 0)
                split_weight(2)
                slices(0, 0, 0, False)
                slices(1, 1, 0, False)
                with dve.Fori(1, NIT - 1) as i:
                    for u in range(2):
                        slices(2 * i + u, u, i, False)
                slices(count - 2, 0, NIT - 1, False)
                slices(count - 1, 1, NIT - 1, True)
                for j in range(J):
                    add(count - 1, j, 1, NIT - 1)

            @block.tensor
            def _(pe):
                def turn(c, u, i):
                    pe.wait_ge(xn_in[u], 16 * i + 16)
                    if positive(c):
                        pe.wait_ge(lo_ok, c)
                    for k in range(KD):
                        for j in range(J):
                            last = pe.transpose(psT[k][:, j * P:(j + 1) * P], xn[u][:, j, k * P:(k + 1) * P], ident[:])
                    last.then_inc(t_ok, 1)

                def down(c, u):
                    pe.wait_ge(hlo_ok, KI * c + KI)
                    for j in range(J):
                        if positive(J * c + j - 1):
                            pe.wait_ge(y_ok, J * c + j - 1)
                        js = slice(j * P, (j + 1) * P)
                        g = 0
                        for k in range(KI):
                            for t, w in ((h_hi, w_hi), (h_hi, w_lo), (h_lo, w_hi)):
                                last = pe.matmul(psO[j % 2][:, 0:D], t[u][:, k, js], w[2][:, k, :], start=(g == 0),
                                                 stop=(g == 3 * KI - 1))
                                g += 1
                        last.then_inc(o_ps, 1)

                def slices(c, u, i, last_chunk):
                    pe.wait_ge(lo_ok, c + 1)
                    for m in range(KI):
                        if positive(KI * c + m - 1):
                            pe.wait_ge(h_ok, KI * c + m - 1)
                        ms = slice(m * P, (m + 1) * P)
                        for n, dst, done in ((0, psG[m % 2], g_ps), (1, psU[m % 2], gu_ps)):
                            g = 0
                            for k in range(KD):
                                for w, t in ((w_hi, xT_hi), (w_hi, xT_lo), (w_lo, xT_hi)):
                                    last = pe.matmul(dst[:], w[n][:, k, ms], t[u][:, k, :], start=(g == 0),
                                                     stop=(g == 3 * KD - 1))
                                    g += 1
                            last.then_inc(done, 1)
                        if m == 0 and positive(c):
                            down(c - 1, 1 - u)
                        if m == KI - 2 and not last_chunk:
                            turn(c + 1, 1 - u, i + u)

                turn(0, 0, 0)
                pe.wait_ge(w_ok, 3)
                slices(0, 0, 0, False)
                slices(1, 1, 0, False)
                with pe.Fori(1, NIT - 1) as i:
                    for u in range(2):
                        slices(2 * i + u, u, i, False)
                slices(count - 2, 0, NIT - 1, False)
                slices(count - 1, 1, NIT - 1, True)
                down(count - 1, 1)


def routed_ffn(nc, s, tag, grouped_d, routed_d, gate_w, up_w, down_w, tile_run, run_expert, run_end, more_quads, ident):
    with ExitStack() as ctx:
        taken = semaphores(nc, ctx)

        def sb(name, shape, dt=F32):
            return ctx.enter_context(nc.sbuf_tensor(f"{tag}_{name}", shape, dt))

        def ps(name, shape):
            return ctx.enter_context(nc.psum_tensor(f"{tag}_{name}", shape, F32))

        def sem(name):
            return taken(f"{tag}_{name}")

        KD, D, KI, I, E, NRT = s.KD, s.D, s.KI, s.I, s.E, s.NRT
        WG, WU, WD, WN = 0, KD * I, 2 * KD * I, 2 * KD * I + KI * D
        raw = [sb(f"raw{v}", [P, WN]) for v in range(2)]
        w_hi = sb("w_hi", [P, 2 * WN], F32R)
        w_lo = sb("w_lo", [P, 2 * WN], F32R)
        x = [sb(f"x{u}", [P, D]) for u in range(4)]
        xT_hi = [sb(f"xT_hi{u}", [P, D], F32R) for u in range(2)]
        xT_lo = [sb(f"xT_lo{u}", [P, D], F32R) for u in range(2)]
        act_g = [sb(f"act_g{u}", [P, I]) for u in range(2)]
        h = [sb(f"h{u}", [P, I]) for u in range(2)]
        hT_hi = [sb(f"hT_hi{u}", [P, I], F32R) for u in range(2)]
        hT_lo = [sb(f"hT_lo{u}", [P, I], F32R) for u in range(2)]
        o = [sb(f"o{u}", [P, D]) for u in range(4)]
        psX = ps("psX", [P, 512])
        psG = ps("psG", [P, I])
        psU = ps("psU", [P, I])
        psH = ps("psH", [P, I])
        psO = [ps(f"psO{u}", [P, 512]) for u in range(2)]

        raw_in = [sem(f"raw_in{v}") for v in range(2)]
        split_ok = sem("split_ok")
        pool_passed = sem("pool_passed")
        sp_passed = sem("sp_passed")
        hi_w_ok = sem("hi_w_ok")
        x_in = [sem(f"x_in{u}") for u in range(4)]
        x_t = sem("x_t")
        xhi_ok = sem("xhi_ok")
        xlo_ok = sem("xlo_ok")
        g_ps = sem("g_ps")
        gu_ps = sem("gu_ps")
        act_ok = sem("act_ok")
        h_ok = sem("h_ok")
        h_t = sem("h_t")
        hhi_ok = sem("hhi_ok")
        hlo_ok = sem("hlo_ok")
        o_ps = sem("o_ps")
        o_ok = sem("o_ok")
        o_out = [sem(f"o_out{u}") for u in range(4)]

        x_v = grouped_d.rearrange("(t p) d -> t p d", p=P)
        o_v = routed_d.rearrange("(t p) d -> t p d", p=P)
        NIT, SURE = NRT // 4, s.NTL // 4

        def the_rest(eng, four):
            had = eng.value_load(more_quads[0:1, 0:1], min_val=0, max_val=NIT - SURE) + SURE
            with eng.Fori(SURE, NIT) as i:
                with eng.If(i < had):
                    four(i)
            return had

        with nc.Block() as block:
            @block.sync
            def _(sp):
                def load(t, u):
                    sp.dma_start(x[u][:], x_v[ds(t, 1)].rearrange("o p d -> (o p) d")).then_inc(x_in[u], 16)

                def store(t, u):
                    sp.wait_ge(o_ok, t + 1)
                    sp.dma_start(o_v[ds(t, 1)].rearrange("o p d -> (o p) d"), o[u][:]).then_inc(o_out[u], 16)

                for u in range(4):
                    load(u, u)

                def four(i):
                    for u in range(4):
                        sp.wait_ge(x_t, 4 * i - 3 + u)
                        load(4 * i + u, u)
                        store(4 * i - 4 + u, u)

                with sp.Fori(1, SURE) as i:
                    four(i)
                had = the_rest(sp, four)
                for u in range(4):
                    store(4 * had - 4 + u, u)
                for u in range(4):
                    sp.wait_ge(o_out[u], 16 * had)
                hold(sp, sp_passed)

            @block.gpsimd
            def _(pool):
                def load(r, v):
                    e = pool.value_load(run_expert[0:1, ds(r, 1)], min_val=0, max_val=E - 1)
                    for w, at, k in ((gate_w, WG, KD), (up_w, WU, KD), (down_w, WD, KI)):
                        n = w.shape[2]
                        pool.dma_start(raw[v][:, at:at + k * n].rearrange("p (k n) -> p k n", k=k),
                                       w[ds(e, 1)].rearrange("o (k p) n -> p (o k) n", p=P)).then_inc(raw_in[v], 16)

                def split(r, v, j, wait_tiles):
                    pool.wait_ge(raw_in[v], 48 * j + 48)
                    if wait_tiles:
                        ended = pool.value_load(run_end[0:1, ds(r - 2, 1)], min_val=1, max_val=NRT + 1)
                        pool.wait_ge(o_ps, ended)
                        hold(pool, pool_passed)
                    hi = w_hi[:, v * WN:(v + 1) * WN]
                    pool.tensor_scalar(hi, raw[v][:], 1.0, 0.0, ALU.mult, ALU.add).then_inc(hi_w_ok, 1)
                    pool.wait_ge(hi_w_ok, r + 1)
                    pool.tensor_tensor(w_lo[:, v * WN:(v + 1) * WN], raw[v][:], hi.bitcast(F32), ALU.subtract).then_inc(split_ok, 1)

                pool.sem_inc(o_ps, 1)
                load(0, 0)
                load(1, 1)
                for v in range(2):
                    split(v, v, 0, False)
                    pool.wait_ge(split_ok, v + 1)
                    load(2 + v, v)
                with pool.Fori(1, E // 2 - 1) as j:
                    for v in range(2):
                        split(2 * j + v, v, j, True)
                        pool.wait_ge(split_ok, 2 * j + v + 1)
                        load(2 * j + 2 + v, v)
                for v in range(2):
                    split(E - 2 + v, v, E // 2 - 1, True)

            @block.scalar
            def _(act):
                def x_hi(t, u):
                    act.wait_ge(x_t, t + 1)
                    if positive(t - 1):
                        act.wait_ge(gu_ps, t - 1)
                    act.copy(xT_hi[u % 2][:], psX[:, 0:D]).then_inc(xhi_ok, 1)

                def gate(t, u):
                    act.wait_ge(g_ps, t + 1)
                    if positive(t - 1):
                        act.wait_ge(h_ok, t - 1)
                    act.activation(act_g[u % 2][:], psG[:], ACT.Silu).then_inc(act_ok, 1)

                def h_hi(t, u):
                    act.wait_ge(h_t, t + 1)
                    if positive(t - 1):
                        act.wait_ge(o_ps, t)
                    act.copy(hT_hi[u % 2][:], psH[:]).then_inc(hhi_ok, 1)

                def half(t, u, i):
                    act.wait_ge(o_ps, t + 2)
                    if positive(i):
                        act.wait_ge(o_out[u], 16 * i)
                    act.mul(o[u][:], psO[u % 2][:, 0:D], 0.5).then_inc(o_ok, 1)

                def tile(t, u, i, ahead=True):
                    if positive(t):
                        h_hi(t - 1, (u - 1) % 4)
                    gate(t, u)
                    if ahead:
                        x_hi(t + 1, (u + 1) % 4)
                    if positive(t):
                        half(t - 1, (u - 1) % 4, i - 1 if u == 0 else i)

                x_hi(0, 0)
                for u in range(4):
                    tile(u, u, 0)
                with act.Fori(1, SURE - 1) as i:
                    for u in range(4):
                        tile(4 * i + u, u, i)
                for u in range(4):
                    tile(4 * SURE - 4 + u, u, SURE - 1, ahead=u < 3)

                def four(i):
                    x_hi(4 * i, 0)
                    for u in range(4):
                        tile(4 * i + u, u, i, ahead=u < 3)

                had = the_rest(act, four)
                h_hi(4 * had - 1, 3)
                half(4 * had - 1, 3, had - 1)

            @block.vector
            def _(dve):
                def x_lo(t, u):
                    dve.wait_ge(xhi_ok, t + 1)
                    dve.tensor_tensor(xT_lo[u % 2][:], psX[:, 0:D], xT_hi[u % 2][:].bitcast(F32), ALU.subtract).then_inc(xlo_ok, 1)

                def mul(t, u):
                    dve.wait_ge(act_ok, t + 1)
                    dve.wait_ge(gu_ps, t + 1)
                    if positive(t - 1):
                        dve.wait_ge(h_t, t - 1)
                    dve.tensor_tensor(h[u % 2][:], act_g[u % 2][:], psU[:], ALU.mult).then_inc(h_ok, 1)

                def h_lo(t, u):
                    dve.wait_ge(hhi_ok, t + 1)
                    dve.tensor_tensor(hT_lo[u % 2][:], psH[:], hT_hi[u % 2][:].bitcast(F32), ALU.subtract).then_inc(hlo_ok, 1)

                def tile(t, u, ahead=True):
                    if positive(t):
                        h_lo(t - 1, (u - 1) % 4)
                    mul(t, u)
                    if ahead:
                        x_lo(t + 1, (u + 1) % 4)

                x_lo(0, 0)
                for u in range(4):
                    tile(u, u)
                with dve.Fori(1, SURE - 1) as i:
                    for u in range(4):
                        tile(4 * i + u, u)
                for u in range(4):
                    tile(4 * SURE - 4 + u, u, ahead=u < 3)

                def four(i):
                    x_lo(4 * i, 0)
                    for u in range(4):
                        tile(4 * i + u, u, ahead=u < 3)

                had = the_rest(dve, four)
                h_lo(4 * had - 1, 3)

            @block.tensor
            def _(pe):
                def turn_x(t, u, i):
                    pe.wait_ge(x_in[u], 16 * i + 16)
                    if positive(t):
                        pe.wait_ge(xlo_ok, t)
                    for k in range(KD):
                        last = pe.transpose(psX[:, k * P:(k + 1) * P], x[u][:, k * P:(k + 1) * P], ident[:])
                    last.then_inc(x_t, 1)

                def gate_up(t, u, slot):
                    pe.wait_ge(xlo_ok, t + 1)
                    if positive(t):
                        pe.wait_ge(h_ok, t)
                    for at, dst, done in ((WG, psG, g_ps), (WU, psU, gu_ps)):
                        g = 0
                        for k in range(KD):
                            for xT, w in ((xT_hi, w_hi), (xT_lo, w_hi), (xT_hi, w_lo)):
                                last = pe.matmul(dst[:], xT[u % 2][:, k * P:(k + 1) * P], w[:, ds(slot * WN + (at + k * I), I)],
                                                 start=(g == 0), stop=(g == 3 * KD - 1))
                                g += 1
                        last.then_inc(done, 1)

                def turn_h(t, u):
                    pe.wait_ge(h_ok, t + 1)
                    if positive(t):
                        pe.wait_ge(hlo_ok, t)
                    for k in range(KI):
                        last = pe.transpose(psH[:, k * P:(k + 1) * P], h[u % 2][:, k * P:(k + 1) * P], ident[:])
                    last.then_inc(h_t, 1)

                def down(t, u, slot):
                    pe.wait_ge(hlo_ok, t + 1)
                    if positive(t - 1):
                        pe.wait_ge(o_ok, t - 1)
                    g = 0
                    for k in range(KI):
                        for hT, w in ((hT_hi, w_hi), (hT_lo, w_hi), (hT_hi, w_lo)):
                            last = pe.matmul(psO[u % 2][:, 0:D], hT[u % 2][:, k * P:(k + 1) * P], w[:, ds(slot * WN + (WD + k * D), D)],
                                             start=(g == 0), stop=(g == 3 * KI - 1))
                            g += 1
                    last.then_inc(o_ps, 1)

                def run_of(t):
                    return pe.value_load(tile_run[0:1, ds(t, 1)], min_val=0, max_val=E - 1)

                def slot_of(r):
                    return pe.snap(r % 2, min_val=0, max_val=1)

                def tile(t, u, i, ahead=True):
                    r = run_of(t)
                    slot = slot_of(r)
                    if positive(t):
                        slot_before = slot_of(run_of(t - 1))
                        turn_h(t - 1, (u - 1) % 4)
                    pe.wait_ge(split_ok, r + 1)
                    gate_up(t, u, slot)
                    if ahead:
                        turn_x(t + 1, (u + 1) % 4, i + 1 if u == 3 else i)
                    if positive(t):
                        down(t - 1, (u - 1) % 4, slot_before)

                turn_x(0, 0, 0)
                for u in range(4):
                    tile(u, u, 0)
                with pe.Fori(1, SURE - 1) as i:
                    for u in range(4):
                        tile(4 * i + u, u, i)
                for u in range(4):
                    tile(4 * SURE - 4 + u, u, SURE - 1, ahead=u < 3)

                def four(i):
                    turn_x(4 * i, 0, i)
                    for u in range(4):
                        tile(4 * i + u, u, i, ahead=u < 3)

                had = the_rest(pe, four)
                turn_h(4 * had - 1, 3)
                down(4 * had - 1, 3, slot_of(run_of(4 * had - 1)))


def attention(nc, s, y_d, routed_d, out_d, stack_d, w_inT, b_in, w_outT, b_out, place, ident, zeros):
    with ExitStack() as ctx:
        taken = semaphores(nc, ctx)

        def sb(name, shape, dt=F32):
            return ctx.enter_context(nc.sbuf_tensor(f"at_{name}", shape, dt))

        def ps(name, shape):
            return ctx.enter_context(nc.psum_tensor(f"at_{name}", shape, F32))

        def sem(name):
            return taken(f"at_{name}")

        J, KD, D, B, T, H, HD = s.J, s.KD, s.D, s.B, s.T, s.H, s.HD
        STEPS, QUAD = 16, 4
        HG = P // HD
        VW = P + HD
        SCALE = float(HD) ** -0.5

        def keys(qt):
            return list(range(max(0, qt - 1), min(J - 1, qt + 1) + 1))

        def units(st):
            return len(keys(st // 4))

        UNITS = sum(units(st) for st in range(STEPS))
        unit_at = [sum(units(x) for x in range(st)) for st in range(STEPS + 1)]

        def by_act(n):
            return n == 2
        act_at = [sum(by_act(n) for x in range(st) for n in range(units(x))) for st in range(STEPS + 1)]
        dve_at = [unit_at[st] - act_at[st] for st in range(STEPS + 1)]

        w_hi = sb("w_hi", [P, KD, 3 * D], F32R)
        w_lo = sb("w_lo", [P, KD, 3 * D], F32R)
        wo_hi = sb("wo_hi", [P, KD, D], F32R)
        wo_lo = sb("wo_lo", [P, KD, D], F32R)
        bqk = sb("bqk", [P, 4])
        bv = sb("bv", [P, D])
        bo = sb("bo", [P, D])
        ident_bf = sb("ident_bf", [P, P], BF16)
        mask = sb("mask", [P, 2, P], BF16)

        q_st = sb("q_st", [P, H, T], F32R)
        k_st = [sb(f"k_st{v}", [P, H // 2, T], F32R) for v in range(2)]
        v_dg = sb("v_dg", [P, J, 2, HG * VW])
        prob = [sb(f"prob{v}", [P, QUAD, 3 * P]) for v in range(2)]
        probT = [sb(f"probT{v}", [P, 12 * P]) for v in range(2)]
        xT_hi = sb("xT_hi", [P, KD, T], F32R)
        xT_lo = sb("xT_lo", [P, KD, T], F32R)
        pr_hi = [sb(f"pr_hi{v}", [P, T], F32R) for v in range(2)]
        pr_lo = [sb(f"pr_lo{v}", [P, T], F32R) for v in range(2)]
        x = sb("x", [P, J, D])
        r = sb("r", [P, J, D])
        xn = sb("xn", [P, J, D])
        res = [sb(f"res{v}", [P, J, D]) for v in range(2)]
        o = sb("o", [P, J, D])
        place_c = sb("place_c", [P, J], I32)
        stats = sb("stats", [P, J, 6])
        mv = sb("mv", [P, J, 2])
        vare = sb("vare", [P, J])
        rstd = sb("rstd", [P, J])
        neg_half = sb("neg_half", [P, J])
        nmax = [sb(f"nmax{v}", [P, QUAD]) for v in range(2)]
        total = [sb(f"total{v}", [P, H]) for v in range(2)]
        inv = sb("inv", [P, H])
        inv_w = sb("inv_w", [P, D])
        invT = sb("invT", [P, D])
        ctxt = sb("ctxt", [P, D])
        ctx_hi = sb("ctx_hi", [P, D], F32R)
        ctx_lo = sb("ctx_lo", [P, D], F32R)

        place_ok = sem("place_ok")
        r_in = sem("r_in")
        y_in = sem("y_in")
        pool_passed = sem("pool_passed")

        def batch(v, b):
            return v[ds(b, 1)].rearrange("o p j d -> (o p) j d")

        def load(sp, b):
            sp.dma_start(x[:], batch(y_d.rearrange("(c j p) d -> c p j d", j=J, p=P), b)).then_inc(y_in, 16)

        def fetch(pool, b):
            pool.tensor_copy(place_c[:], place[:, ds(b * J, J)]).then_inc(place_ok, 1)
            pool.wait_ge(place_ok, b + 1)
            hold(pool, pool_passed)
            for j in range(J):
                pool.indirect_dma_start(out=r[:, j, :], out_offset=None, in_=routed_d,
                                        in_offset=bass.IndirectOffsetOnAxis(ap=place_c[:, j:j + 1], axis=0)
                                        ).then_inc(r_in, 16)

        with (
            nc.sbuf_tensor("at_w_raw", [P, KD, 3 * D], F32) as w_raw,
            nc.sbuf_tensor("at_wo_raw", [P, KD, D], F32) as wo_raw,
            nc.sbuf_tensor("at_bqk_raw", [P, 4], F32) as bqk_raw,
            nc.Block() as block,
        ):
            in_ = sem("w_in")
            pre = sem("pre")
            chain = sem("w_chain")

            @block.sync
            def _(sp):
                sp.dma_start(w_raw[:], w_inT.rearrange("(k p) n -> p k n", p=P)).then_inc(in_, 16)
                sp.dma_start(wo_raw[:], w_outT.rearrange("(k p) n -> p k n", p=P)).then_inc(in_, 16)
                for n, at in enumerate((0, D, P, D + P)):
                    sp.dma_start(bqk_raw[:, n:n + 1], b_in[at:at + P].rearrange("(p o) -> p o", o=1)).then_inc(in_, 16)
                sp.dma_start(bv[:], b_in[2 * D:3 * D].rearrange("(o n) -> o n", o=1).broadcast_to([P, D])).then_inc(in_, 16)
                sp.dma_start(bo[:], b_out.rearrange("(o n) -> o n", o=1).broadcast_to([P, D])).then_inc(in_, 16)
                load(sp, 0)
                sp.wait_ge(in_, 16 * 8)

            @block.scalar
            def _(act):
                for j in range(J):
                    act.copy(v_dg[:, j].rearrange("p g (r c) -> p (g r) c", c=VW),
                             zeros[:, 0:VW].unsqueeze(1).broadcast_to([P, 2 * HG, VW]))

            @block.gpsimd
            def _(pool):
                pool.memset(ident_bf[:], 0.0).then_inc(pre, 1)
                pool.memset(mask[:], 0.0).then_inc(pre, 1)
                pool.wait_ge(pre, 2)
                pool.affine_select(out=ident_bf[:], in_=ident_bf[:], compare_op=ALU.not_equal, fill=1.0, base=0,
                                   pattern=[[-1, P]], channel_multiplier=1)
                pool.affine_select(out=mask[:, 0, :], in_=mask[:, 0, :], compare_op=ALU.is_ge, fill=NEG, base=P - WINDOW,
                                   pattern=[[1, P]], channel_multiplier=-1)
                pool.affine_select(out=mask[:, 1, :], in_=mask[:, 1, :], compare_op=ALU.is_ge, fill=NEG, base=WINDOW - P,
                                   pattern=[[-1, P]], channel_multiplier=1)
                fetch(pool, 0)
                pool.memset(neg_half[:], -0.5)
                pool.memset(k_st[0][:].bitcast(F32), 0.0)
                pool.memset(k_st[1][:].bitcast(F32), 0.0)

            @block.vector
            def _(dve):
                dve.memset(q_st[:].bitcast(F32), 0.0)
                dve.wait_ge(in_, 16 * 8)
                dve.tensor_scalar(w_raw[:, :, 0:D], w_raw[:, :, 0:D], SCALE, None, ALU.mult).then_inc(chain, 1)
                dve.wait_ge(chain, 1)
                dve.tensor_copy(w_hi[:], w_raw[:]).then_inc(chain, 1)
                dve.tensor_copy(wo_hi[:], wo_raw[:]).then_inc(chain, 1)
                dve.tensor_copy(bqk[:], bqk_raw[:]).then_inc(chain, 1)
                dve.wait_ge(chain, 4)
                dve.tensor_tensor(w_lo[:], w_raw[:], w_hi[:].bitcast(F32), ALU.subtract)
                dve.tensor_tensor(wo_lo[:], wo_raw[:], wo_hi[:].bitcast(F32), ALU.subtract)
                for n in (0, 2):
                    dve.tensor_scalar(bqk[:, n:n + 1], bqk_raw[:, n:n + 1], SCALE, None, ALU.mult)

        psS = [ps(f"psS{v}", [P, 2, 512]) for v in range(2)]
        psT = [ps(f"psT{v}", [P, 512]) for v in range(2)]
        psC = ps("psC", [P, 512])
        psM = ps("psM", [P, 512])

        s_ps = sem("s_ps")
        mx_ok = sem("mx_ok")
        ex_ok = sem("ex_ok")
        t_ps = sem("t_ps")
        pta_ok = sem("pta_ok")
        ptv_ok = sem("ptv_ok")
        pv_ok = sem("pv_ok")
        inv_ok = sem("inv_ok")
        invw_ok = sem("invw_ok")
        i_ps = sem("i_ps")
        invT_ok = sem("invT_ok")
        c_ok = sem("c_ok")
        chi_ok = sem("chi_ok")
        clo_ok = sem("clo_ok")
        o_ps = sem("o_ps")
        o_ok = sem("o_ok")
        o_out = sem("o_out")
        x_ok = sem("x_ok")
        stat_ok = sem("stat_ok")
        vare_ok = sem("vare_ok")
        rstd_ok = sem("rstd_ok")
        xn_ok = sem("xn_ok")
        sum_ok = sem("sum_ok")
        res_ok = sem("res_ok")
        x_ps = sem("x_ps")
        xhi_ok = sem("xhi_ok")
        xlo_ok = sem("xlo_ok")
        p_ps = sem("p_ps")
        phi_ok = sem("phi_ok")
        plo_ok = sem("plo_ok")
        spill = [sem(f"spill{n}") for n in range(4)]
        stacked = [sem(f"stacked{n}") for n in range(4)]
        q_late = [sem(f"q_late{m}") for m in range(2)]
        v_ps = sem("v_ps")
        v_ok = sem("v_ok")
        dve_passed = sem("dve_passed")

        def view(d):
            return d.rearrange("(c j p) d -> c p j d", j=J, p=P)

        out_v = view(out_d)

        A_JOBS = {1: ("v", 2, 0), 3: ("v", 3, 0), 4: ("x", 0, 1), 5: ("x", 1, 1), 6: ("p", 0, 1), 7: ("p", 1, 1),
                  8: ("p", 2, 1), 9: ("p", 3, 1), 10: ("v", 0, 1), 13: ("v", 1, 1)}
        B_JOBS = {st: ("i", st // 4 - 1, 0) for st in range(0, 16, 4)} | {st: ("o", st // 4 - 1, 0) for st in range(2, 16, 4)}

        def jobs(b, first, last):
            found = []
            for st in range(STEPS):
                if st in A_JOBS:
                    kind, n, ahead = A_JOBS[st]
                    if not (ahead and last):
                        found.append((st, "a", kind, n, b + ahead))
                if st in B_JOBS:
                    kind, n, _ = B_JOBS[st]
                    if n >= 0:
                        found.append((st, "b", kind, n, b))
                    elif not first:
                        found.append((st, "b", kind, J - 1, b - 1))
            return found

        def job_done(kind, n, b):
            return {"v": (v_ok, J * b + n + 1), "x": (xlo_ok, KD * b + n + 1), "p": (plo_ok, 4 * b + n + 1),
                    "i": (invT_ok, J * b + n + 1), "o": (o_ok, J * b + n + 1)}[kind]

        AHEAD = [("x", 0), ("x", 1), ("p", 0), ("p", 1), ("p", 2), ("p", 3), ("v", 0), ("v", 1)]

        def each_batch(eng, body):
            body(0, 0, True, False)
            body(1, 1, False, False)
            with eng.Fori(1, B // 2 - 1) as i:
                for v in range(2):
                    body(2 * i + v, v, False, False)
            body(B - 2, 0, False, False)
            body(B - 1, 1, False, True)

        with nc.Block() as block:
            @block.sync
            def _(sp):
                def stack(n, b, v):
                    side, m = n % 2, n // 2
                    read, spilled, scored = (ahead_of_wait(sp, value) for value in (96 * b, 32 * b + 32, 2 * STEPS * b - STEPS))
                    sp.wait_ge(plo_ok, 4 * b + n + 1)
                    if positive(b):
                        sp.wait_ge(stacked[n], read)
                        if side == 0:
                            sp.wait_ge(q_late[m], read)
                    rows = slice(m * P, (m + 1) * P)
                    sp.dma_start(stack_d[side, 0, rows, :], pr_hi[n % 2][:].bitcast(F32)).then_inc(spill[n], 16)
                    sp.dma_start(stack_d[side, 1, rows, :], pr_lo[n % 2][:].bitcast(F32)).then_inc(spill[n], 16)
                    sp.wait_ge(spill[n], spilled)
                    if side == 0:
                        if positive(2 * STEPS * b):
                            sp.wait_ge(s_ps, scored)
                        q_rows(m, 0, stacked[n])
                        return
                    for at_row, part in enumerate((0, 1, 0)):
                        src = stack_d[1, part, rows, :].rearrange("(h e d) t -> e d h t", e=2, d=HD)
                        for e in range(2):
                            at = 64 * e + HD * at_row
                            dst = k_st[v][at:at + HD, m * HG // 2:(m + 1) * HG // 2, :]
                            sp.dma_start(dst.bitcast(F32), src[e]).then_inc(stacked[n], 16)

                def q_rows(m, half, landed):
                    ts = slice(half * T // 2, (half + 1) * T // 2)
                    for at_row, part in enumerate((0, 0, 1)):
                        src = stack_d[0, part, m * P:(m + 1) * P, ts].rearrange("(h e d) t -> e d h t", e=2, d=HD)
                        for e in range(2):
                            at = 64 * e + HD * at_row
                            dst = q_st[at:at + HD, m * HG + e:(m + 1) * HG:2, ts]
                            sp.dma_start(dst.bitcast(F32), src[e]).then_inc(landed, 16)

                def q_second(b):
                    if positive(2 * STEPS * b):
                        sp.wait_ge(s_ps, 2 * STEPS * b)
                    for m in range(2):
                        q_rows(m, 1, q_late[m])

                def store(b):
                    sp.wait_ge(o_ok, J * b + J)
                    sp.dma_start(batch(out_v, b), o[:]).then_inc(o_out, 16)

                def body(b, v, first, last):
                    q_second(b)
                    if not first:
                        store(b - 1)
                    if not last:
                        if not (isinstance(b, int) and b + 2 >= B):
                            sp.wait_ge(sum_ok, b + 2)
                            load(sp, b + 2)
                        for n in range(4):
                            stack(n, b + 1, 1 - v)

                for n in range(4):
                    stack(n, 0, 0)
                sp.wait_ge(sum_ok, 1)
                load(sp, 1)
                each_batch(sp, body)
                store(B - 1)
                sp.wait_ge(o_out, 16 * B)

            @block.gpsimd
            def _(pool):
                def ahead(b, v, more):
                    pool.wait_ge(y_in, 16 * b + 16)
                    pool.wait_ge(r_in, 16 * J * b + 16 * J)
                    pool.tensor_tensor(x[:], x[:], r[:], ALU.add).then_inc(x_ok, 1)
                    pool.wait_ge(x_ok, b + 1)
                    if more:
                        fetch(pool, b + 1)
                    pool.wait_ge(vare_ok, b + 1)
                    pool.tensor_tensor(rstd[:], vare[:], neg_half[:], ALU.pow).then_inc(rstd_ok, 1)
                    pool.wait_ge(xn_ok, b + 1)
                    if positive(J * b - J):
                        pool.wait_ge(o_ok, J * b - J)
                    pool.tensor_tensor(res[v][:], x[:], xn[:], ALU.add).then_inc(sum_ok, 1)
                    pool.wait_ge(sum_ok, b + 1)
                    pool.tensor_tensor(res[v][:], res[v][:], bo[:].unsqueeze(1).broadcast_to([P, J, D]), ALU.add).then_inc(res_ok, 1)

                ahead(0, 0, True)

                def body(b, v, first, last):
                    if not last:
                        ahead(b + 1, 1 - v, not (isinstance(b, int) and b + 2 >= B))

                each_batch(pool, body)

            @block.scalar
            def _(act):
                def job(kind, n, b):
                    if kind == "x":
                        act.wait_ge(x_ps, KD * b + n + 1)
                        if n == 0 and positive(J * b):
                            act.wait_ge(v_ps, J * b)
                        act.copy(xT_hi[:, n, :], psM[:]).then_inc(xhi_ok, 1)
                    elif kind == "p":
                        act.wait_ge(p_ps, 4 * b + n + 1)
                        if n >= 2:
                            act.wait_ge(spill[n - 2], 32 * b + 32)
                        elif positive(b):
                            act.wait_ge(spill[n + 2], 32 * b)
                        act.activation(pr_hi[n % 2][:], psM[:], ACT.Identity, bias=bqk[:, n:n + 1]).then_inc(phi_ok, 1)
                    elif kind == "i":
                        act.wait_ge(i_ps, J * b + n + 1)
                        if positive(J * b + n):
                            act.wait_ge(c_ok, J * b + n)
                        act.copy(invT[:], psM[:, 0:D]).then_inc(invT_ok, 1)

                def context_hi(n, b):
                    act.wait_ge(c_ok, J * b + n + 1)
                    if positive(J * b + n):
                        act.wait_ge(o_ps, J * b + n)
                    act.copy(ctx_hi[:], ctxt[:]).then_inc(chi_ok, 1)

                def exps(b, st, pairs=(0, 1)):
                    v, qt = st % 2, st // 4
                    w = len(keys(qt)) * P
                    for pr in pairs:
                        act.wait_ge(mx_ok, 2 * STEPS * b + 2 * st + pr + 1)
                        if positive(STEPS * b + st - 1) and pr == 0:
                            act.wait_ge(t_ps, UNITS * b + unit_at[st] - units(st - 1))
                        if st % 4 == 0 and pr == 0 and positive(J * b + qt - 1):
                            act.wait_ge(inv_ok, J * b + qt - 1)
                        for h in range(2 * pr, 2 * pr + 2):
                            head = QUAD * (st % 4) + h
                            last = act.activation(prob[v][:, h, 0:w], psS[pr][:, h % 2, 0:w], ACT.Exp, bias=nmax[v][:, h:h + 1],
                                                  accum_out=total[qt % 2][:, head:head + 1])
                        last.then_inc(ex_ok, 1)

                def copy_out(b, st):
                    for n in range(units(st)):
                        if by_act(n):
                            act.wait_ge(t_ps, UNITS * b + unit_at[st] + n + 1)
                            if positive(STEPS * b + st - 1):
                                act.wait_ge(pv_ok, STEPS * b + st - 1)
                            act.copy(probT[st % 2][:, n * 512:(n + 1) * 512], psT[(unit_at[st] + n) % 2][:]).then_inc(pta_ok, 1)

                def body(b, v, first, last):
                    todo = jobs(b, first, last)
                    for st in range(STEPS):
                        for st_, where, kind, n, bb in todo:
                            if (st_, where) == (st - 1, "b"):
                                job(kind, n, bb)
                        ahead = (b, st + 1) if st + 1 < STEPS else (b + 1, 0)
                        if st + 1 < STEPS or not last:
                            exps(*ahead, pairs=(0,))
                        for st_, where, kind, n, bb in todo:
                            if (st_, where) == (st, "a"):
                                job(kind, n, bb)
                            if (st_, where, kind) == (st - 1, "b", "i"):
                                context_hi(n, bb)
                        if st + 1 < STEPS or not last:
                            exps(*ahead, pairs=(1,))
                        copy_out(b, st)

                for kind, n in AHEAD:
                    job(kind, n, 0)
                exps(0, 0)
                each_batch(act, body)
                job("i", J - 1, B - 1)
                context_hi(J - 1, B - 1)

            @block.vector
            def _(dve):
                def norm(b, v):
                    dve.wait_ge(x_ok, b + 1)
                    for j in range(J):
                        last = dve.bn_stats(stats[:, j, :], x[:, j, :])
                    last.then_inc(stat_ok, 1)
                    dve.wait_ge(stat_ok, 2 * b + 1)
                    hold(dve, dve_passed)
                    for j in range(J):
                        last = dve.bn_aggr(mv[:, j, :], stats[:, j, :])
                    last.then_inc(stat_ok, 1)
                    dve.wait_ge(stat_ok, 2 * b + 2)
                    dve.tensor_scalar(vare[:], mv[:, :, 1], EPS, None, ALU.add).then_inc(vare_ok, 1)

                def scale(b, v):
                    dve.wait_ge(rstd_ok, b + 1)
                    if positive(KD * b):
                        dve.wait_ge(x_ps, KD * b)
                        dve.wait_ge(sum_ok, b)
                    for j in range(J):
                        last = dve.tensor_scalar(xn[:, j, :], x[:, j, :], mv[:, j, 0:1], rstd[:, j:j + 1], ALU.subtract, ALU.mult)
                    last.then_inc(xn_ok, 1)

                def job(kind, n, b, v):
                    if kind == "x":
                        dve.wait_ge(xhi_ok, KD * b + n + 1)
                        dve.tensor_tensor(xT_lo[:, n, :], psM[:], xT_hi[:, n, :].bitcast(F32), ALU.subtract).then_inc(xlo_ok, 1)
                    elif kind == "p":
                        dve.wait_ge(phi_ok, 4 * b + n + 1)
                        dve.scalar_tensor_tensor(pr_lo[n % 2][:], psM[:], bqk[:, n:n + 1], pr_hi[n % 2][:].bitcast(F32),
                                                 ALU.add, ALU.subtract).then_inc(plo_ok, 1)
                    elif kind == "v":
                        dve.wait_ge(v_ps, J * b + n + 1)
                        if positive(STEPS * b):
                            dve.wait_ge(pv_ok, STEPS * (b - 1) + 4 * min(n + 2, J))
                        dve.tensor_tensor(v_dg[:, n].rearrange("p g (h c) -> p g h c", c=VW)[:, :, :, 0:HD],
                                          psM[:, 0:D].rearrange("p (g h d) -> p g h d", g=2, d=HD),
                                          bv[:].rearrange("p (g h d) -> p g h d", g=2, d=HD), ALU.add).then_inc(v_ok, 1)
                    elif kind == "i":
                        dve.wait_ge(invT_ok, J * b + n + 1)
                        dve.wait_ge(pv_ok, STEPS * b + 4 * n + 4)
                        if positive(J * b + n):
                            dve.wait_ge(clo_ok, J * b + n)
                        dve.tensor_tensor(ctxt[:], psC[:, 0:D], invT[:], ALU.mult).then_inc(c_ok, 1)
                    elif kind == "o":
                        dve.wait_ge(o_ps, J * b + n + 1)
                        if n == 0:
                            dve.wait_ge(res_ok, b + 1)
                            if positive(b):
                                dve.wait_ge(o_out, 16 * b)
                        dve.tensor_tensor(o[:, n, :], psM[:, 0:D], res[v][:, n, :], ALU.add).then_inc(o_ok, 1)

                def context_lo(n, b):
                    dve.wait_ge(chi_ok, J * b + n + 1)
                    dve.tensor_tensor(ctx_lo[:], ctxt[:], ctx_hi[:].bitcast(F32), ALU.subtract).then_inc(clo_ok, 1)

                def maxima(b, st):
                    w = len(keys(st // 4)) * P
                    for pr in range(2):
                        dve.wait_ge(s_ps, 2 * STEPS * b + 2 * st + pr + 1)
                        if positive(2 * STEPS * b + 2 * st + pr - 3):
                            dve.wait_ge(ex_ok, 2 * STEPS * b + 2 * st + pr - 3)
                        dve.tensor_reduce(nmax[st % 2][:, 2 * pr:2 * pr + 2], psS[pr][:, :, 0:w], AX.X, ALU.max,
                                          negate=True).then_inc(mx_ok, 1)

                def copy_out(b, st):
                    for n in range(units(st)):
                        if not by_act(n):
                            dve.wait_ge(t_ps, UNITS * b + unit_at[st] + n + 1)
                            if positive(STEPS * b + st - 1):
                                dve.wait_ge(pv_ok, STEPS * b + st - 1)
                            dve.tensor_copy(probT[st % 2][:, n * 512:(n + 1) * 512], psT[(unit_at[st] + n) % 2][:]).then_inc(ptv_ok, 1)

                def invert(b, qt):
                    dve.wait_ge(ex_ok, 2 * STEPS * b + 8 * qt + 8)
                    dve.reciprocal(inv[:], total[qt % 2][:]).then_inc(inv_ok, 1)
                    dve.wait_ge(inv_ok, J * b + qt + 1)
                    if positive(J * b + qt):
                        dve.wait_ge(i_ps, J * b + qt)
                    dve.tensor_copy(inv_w[:].rearrange("p (h d) -> p h d", d=HD),
                                    inv[:].unsqueeze(2).broadcast_to([P, H, HD])).then_inc(invw_ok, 1)

                def body(b, v, first, last):
                    todo = jobs(b, first, last)
                    def jobs_at(st, place):
                        for st_, where, kind, n, bb in todo:
                            if (st_, where) == (st, place):
                                own = 1 - v if n == J - 1 and kind == "o" else v
                                job(kind, n, bb, own)

                    for st in range(STEPS):
                        jobs_at(st - 1, "b")
                        if st + 1 < STEPS:
                            maxima(b, st + 1)
                        elif not last:
                            maxima(b + 1, 0)
                        copy_out(b, st)
                        jobs_at(st, "a")
                        for st_, _, kind, n, bb in todo:
                            if (st_, kind) == (st - 1, "i"):
                                context_lo(n, bb)
                        if st == 1 and not last:
                            norm(b + 1, 1 - v)
                        if st == 2 and not last:
                            scale(b + 1, 1 - v)
                        if st % 4 == 3:
                            invert(b, st // 4)

                norm(0, 0)
                scale(0, 0)
                for kind, n in AHEAD:
                    job(kind, n, 0, 0)
                maxima(0, 0)
                each_batch(dve, body)
                job("i", J - 1, B - 1, 1)
                context_lo(J - 1, B - 1)
                job("o", J - 1, B - 1, 1)

            @block.tensor
            def _(pe):
                def split3(out, pairs):
                    g = 0
                    for (a_hi, a_lo), (b_hi, b_lo) in pairs:
                        for left, right in ((a_hi, b_hi), (a_hi, b_lo), (a_lo, b_hi)):
                            last = pe.matmul(out, left, right, start=(g == 0), stop=(g == 3 * len(pairs) - 1))
                            g += 1
                    return last

                def job(kind, n, b, before):
                    if before:
                        pe.wait_ge(*job_done(*before))
                    if kind == "x":
                        pe.wait_ge(xn_ok, b + 1)
                        for j in range(J):
                            last = pe.transpose(psM[:, j * P:(j + 1) * P], xn[:, j, n * P:(n + 1) * P], ident[:])
                        last.then_inc(x_ps, 1)
                    elif kind == "p":
                        pe.wait_ge(xlo_ok, KD * b + KD)
                        at = (n % 2) * D + (n // 2) * P
                        split3(psM[:], [((w_hi[:, k, at:at + P], w_lo[:, k, at:at + P]), (xT_hi[:, k, :], xT_lo[:, k, :]))
                                        for k in range(KD)]).then_inc(p_ps, 1)
                    elif kind == "v":
                        pe.wait_ge(xlo_ok, KD * b + KD)
                        ts = slice(n * P, (n + 1) * P)
                        split3(psM[:, 0:D], [((xT_hi[:, k, ts], xT_lo[:, k, ts]), (w_hi[:, k, 2 * D:3 * D], w_lo[:, k, 2 * D:3 * D]))
                                             for k in range(KD)]).then_inc(v_ps, 1)
                    elif kind == "i":
                        pe.wait_ge(invw_ok, J * b + n + 1)
                        for k in range(KD):
                            last = pe.transpose(psM[:, k * P:(k + 1) * P], inv_w[:, k * P:(k + 1) * P], ident[:])
                        last.then_inc(i_ps, 1)
                    elif kind == "o":
                        pe.wait_ge(clo_ok, J * b + n + 1)
                        split3(psM[:, 0:D], [((ctx_hi[:, k * P:(k + 1) * P], ctx_lo[:, k * P:(k + 1) * P]),
                                              (wo_hi[:, k, :], wo_lo[:, k, :])) for k in range(KD)]).then_inc(o_ps, 1)

                def scores(b, st, v):
                    qt, w = st // 4, len(keys(st // 4)) * P
                    if st == 0:
                        for n in range(2):
                            pe.wait_ge(stacked[n], 96 * b + 96)
                    if st == 2:
                        for n in range(2, 4):
                            pe.wait_ge(stacked[n], 96 * b + 96)
                    if st in (8, 10):
                        pe.wait_ge(q_late[(st - 8) // 2], 96 * b + 96)
                    for pr in range(2):
                        if positive(2 * STEPS * b + 2 * st + pr - 1):
                            pe.wait_ge(ex_ok, 2 * STEPS * b + 2 * st + pr - 1)
                        for e in range(2):
                            head = QUAD * (st % 4) + 2 * pr + e
                            pe.matmul(psS[pr][:, e, 0:w], q_st[:, head, qt * P:(qt + 1) * P],
                                      k_st[v][:, head // 2, keys(qt)[0] * P:keys(qt)[0] * P + w], start=True, stop=False)
                            if len(keys(qt)) == 3:
                                edge = psS[pr][:, e, :].rearrange("p (a c) -> p a c", c=2 * P)[:, :, 0:P]
                                last = pe.matmul(edge, ident_bf[:], mask[:], start=False, stop=True)
                            elif qt == 0:
                                last = pe.matmul(psS[pr][:, e, P:2 * P], ident_bf[:], mask[:, 1, :], start=False, stop=True)
                            else:
                                last = pe.matmul(psS[pr][:, e, 0:P], ident_bf[:], mask[:, 0, :], start=False, stop=True)
                        last.then_inc(s_ps, 1)

                def turn(b, st, lots):
                    nk = units(st)
                    for n in lots:
                        u = unit_at[st] + n
                        before = [(x, m) for x in range(st + 1) for m in range(units(x))][u - 2] if u >= 2 else None
                        if before:
                            x, m = before
                            if by_act(m):
                                pe.wait_ge(pta_ok, act_at[STEPS] * b + act_at[x] + 1)
                            else:
                                pe.wait_ge(ptv_ok, dve_at[STEPS] * b + dve_at[x] + m + 1)
                        elif positive(b):
                            pe.wait_ge(ptv_ok, dve_at[STEPS] * b - 1 + u)
                        heads = [(4 * n + i) // nk for i in range(4)]
                        pe.wait_ge(ex_ok, 2 * STEPS * b + 2 * st + heads[-1] // 2 + 1)
                        for i, h in enumerate(heads):
                            k = (4 * n + i) % nk
                            last = pe.transpose(psT[u % 2][:, i * P:(i + 1) * P], prob[st % 2][:, h, k * P:(k + 1) * P], ident[:])
                        last.then_inc(t_ps, 1)

                def sum_v(b, st):
                    qt, nk = st // 4, units(st)
                    if act_at[st + 1]:
                        pe.wait_ge(pta_ok, act_at[STEPS] * b + act_at[st + 1])
                    pe.wait_ge(ptv_ok, dve_at[STEPS] * b + dve_at[st + 1])
                    if st % 4 == 0:
                        pe.wait_ge(v_ok, J * b + min(qt + 2, J))
                        if positive(J * b + qt):
                            pe.wait_ge(c_ok, J * b + qt)
                    g = st % 4 // 2
                    for h in range(QUAD):
                        hg = QUAD * (st % 2) + h
                        for k, kt in enumerate(keys(qt)):
                            last = pe.matmul(psC[:, g * P:(g + 1) * P], v_dg[:, kt, g, hg * P:(hg + 1) * P],
                                             probT[st % 2][:, (h * nk + k) * P:(h * nk + k + 1) * P],
                                             start=(hg == 0 and k == 0), stop=(hg == HG - 1 and k == nk - 1))
                    last.then_inc(pv_ok, 1)

                def body(b, v, first, last):
                    todo = jobs(b, first, last)
                    before = [("v", 1, b)]
                    for st in range(STEPS):
                        if st + 1 < STEPS:
                            scores(b, st + 1, v)
                        elif not last:
                            scores(b + 1, 0, 1 - v)
                        for where in "ab":
                            for st_, where_, kind, n, bb in todo:
                                if (st_, where_) == (st, where):
                                    job(kind, n, bb, before[-1])
                                    before.append((kind, n, bb))
                            if where == "a":
                                turn(b, st, range(2))
                                if st:
                                    sum_v(b, st - 1)
                                elif not first:
                                    sum_v(b - 1, STEPS - 1)
                                turn(b, st, range(2, units(st)))

                before = None
                for kind, n in AHEAD:
                    job(kind, n, 0, before)
                    before = (kind, n, 0)
                scores(0, 0, 0)
                each_batch(pe, body)
                sum_v(B - 1, STEPS - 1)
                job("i", J - 1, B - 1, ("o", J - 2, B - 1))
                job("o", J - 1, B - 1, ("i", J - 1, B - 1))


def constants(nc, ident, ones_bf, upper_bf, zeros):
    with nc.Block() as block:
        clear = nc.alloc_semaphore("const_clear")
        made = nc.alloc_semaphore("const_made")
        cleared = nc.alloc_semaphore("const_cleared")

        @block.gpsimd
        def _(pool):
            pool.memset(ident[:], 0.0).then_inc(clear, 1)
            pool.memset(ones_bf[:], 1.0).then_inc(clear, 1)
            pool.wait_ge(clear, 2)
            pool.affine_select(out=ident[:], in_=ident[:], compare_op=ALU.not_equal, fill=1.0, base=0,
                               pattern=[[-1, P]], channel_multiplier=1).then_inc(made, 1)
            pool.affine_select(out=upper_bf[:], in_=ones_bf[:], compare_op=ALU.is_gt, fill=0.0, base=0,
                               pattern=[[1, P]], channel_multiplier=-1).then_inc(made, 1)
            pool.wait_ge(made, 2)

        @block.vector
        def _(dve):
            dve.memset(zeros[:], 0.0).then_inc(cleared, 1)
            dve.wait_ge(cleared, 1)


def ffn(nc, s, tag, x_d, xn_d, y_d, grouped_d, routed_d, w, place, state, filled, first, out_d=None):
    ident, ones_bf, upper_bf, zeros = state
    with ExitStack() as ctx:
        def sb(name, shape, dt=F32):
            return ctx.enter_context(nc.sbuf_tensor(f"{tag}_{name}", shape, dt))

        score = sb("score", [P, s.NTL])
        tile_run = sb("tile_run", [1, s.NRT], I32)
        run_expert = sb("run_expert", [1, s.E], I32)
        run_end = sb("run_end", [1, s.E], I32)
        more_quads = sb("more_quads", [1, 1], I32)
        with ExitStack() as inner:
            onehot = inner.enter_context(nc.sbuf_tensor(f"{tag}_onehot", [P, s.NTL, s.E], BF16))
            top_logit = inner.enter_context(nc.sbuf_tensor(f"{tag}_top_logit", [P, s.NTL], F32))
            router(nc, s, tag + "r", x_d, xn_d, w["gate_w"], onehot, top_logit, ident,
                   (grouped_d, routed_d[s.NTL * P:, :], zeros, filled) if first else None)
            places(nc, s, tag + "p", onehot, top_logit, score, place, tile_run, run_expert, run_end, more_quads, ones_bf, upper_bf, ident)
        shared_w = (w["shared_gate_w"], w["shared_up_w"], w["shared_down_w"])
        count = s.NCH if out_d is None else s.NCH // 2
        shared_ffn(nc, s, tag + "s", x_d, xn_d, y_d, 0, count, *shared_w, place, ident, scatter=(grouped_d, score, filled))
        routed_ffn(nc, s, tag + "e", grouped_d, routed_d, w["routed_gate_w"], w["routed_up_w"], w["routed_down_w"],
                   tile_run, run_expert, run_end, more_quads, ident)
        if out_d is not None:
            shared_ffn(nc, s, tag + "t", x_d, xn_d, out_d, count, s.NCH - count, *shared_w, place, ident,
                       gather=(y_d, routed_d))


def macaron(nc, ins, out):
    x = ins["x"].rearrange("b t d -> (b t) d")
    s = Shapes(ins["x"], ins["w_inT"], ins["gate_w"], ins["shared_gate_w"], ins["routed_gate_w"])
    out_d = out.rearrange("b t d -> (b t) d")

    def dram(name, rows):
        return nc.dram_tensor(name, [rows, s.D], F32, kind="Internal").ap()

    xn_d, y_d = dram("xn_d", s.N), dram("y_d", s.N)
    grouped_d, routed_d = dram("grouped_d", s.NRT * P), dram("routed_d", s.NRT * P)
    with (
        nc.sbuf_tensor("ident", [P, P], F32) as ident,
        nc.sbuf_tensor("ones_bf", [P, P], BF16) as ones_bf,
        nc.sbuf_tensor("upper_bf", [P, P], BF16) as upper_bf,
        nc.sbuf_tensor("place", [P, s.NTL], I32) as place,
        nc.sbuf_tensor("zeros", [P, s.D], F32) as zeros,
    ):
        constants(nc, ident, ones_bf, upper_bf, zeros)
        state = (ident, ones_bf, upper_bf, zeros)
        filled = nc.alloc_semaphore("filled")
        ffn(nc, s, "f1", x, xn_d, y_d, grouped_d, routed_d, ins, place, state, filled, True)
        stack_d = nc.dram_tensor("stack_d", [2, 2, s.D, s.T], F32, kind="Internal").ap()
        z_d = dram("z_d", s.N)
        attention(nc, s, y_d, routed_d, z_d, stack_d, ins["w_inT"], ins["b_in"], ins["w_outT"], ins["b_out"], place, ident, zeros)
        ffn(nc, s, "f2", z_d, xn_d, y_d, grouped_d, routed_d, ins, place, state, filled, False, out_d)


_NAMES = {"x": "L0_attn_x", "w_inT": "L0_attn_w_in", "b_in": "L0_attn_b_in", "w_outT": "L0_attn_w_out", "b_out": "L0_attn_b_out",
          "gate_w": "L0_ffn_gate_w", "shared_gate_w": "L0_ffn_shared_gate_w", "shared_up_w": "L0_ffn_shared_up_w",
          "shared_down_w": "L0_ffn_shared_down_w", "routed_gate_w": "L0_ffn_routed_gate_w",
          "routed_up_w": "L0_ffn_routed_up_w", "routed_down_w": "L0_ffn_routed_down_w"}


def kernel(**inputs):
    import numpy as _np
    import concourse.bacc as _bacc
    from concourse import mybir as _mybir
    from concourse.bass_utils import run_bass_kernel_spmd as _run

    nc = _bacc.Bacc("TRN2", target_bir_lowering=False, num_devices=1)
    arrays, aps = {}, {}
    for name, given in _NAMES.items():
        a = _np.asarray(inputs[given])
        a = _np.ascontiguousarray(a.T if name.endswith("T") else a)
        arrays[f"in_{name}"] = a
        aps[name] = nc.dram_tensor(f"in_{name}", a.shape, _mybir.dt.from_np(a.dtype), kind="ExternalInput").ap()
    out = nc.dram_tensor("out_0", arrays["in_x"].shape, _mybir.dt.float32, kind="ExternalOutput").ap()
    macaron(nc, aps, out)
    r = _run(nc, [arrays], core_ids=[0])
    return r.results[0]["out_0"]
```
